# Optimizing a Trainium2 kernel written in Bass

```python
import numpy as np
import jax
import jax.numpy as jnp

def _softmax(x, axis=-1):
    return jax.nn.softmax(x, axis=axis)

def _gelu(x):
    return jax.nn.gelu(x, approximate=True)

def _silu(x):
    return jax.nn.silu(x)

def _sigmoid(x):
    return jax.nn.sigmoid(x)

def _layernorm(x, axis=-1, eps=1e-05):
    m = jnp.mean(x, axis=axis, keepdims=True)
    v = jnp.var(x, axis=axis, keepdims=True)
    return (x - m) / jnp.sqrt(v + eps)

def _scatter_add(tgt, idx, src, axis=0):
    return tgt.at[idx].add(src)

def _segment_sum(src, seg, n):
    return jax.ops.segment_sum(src, seg, n)
kernel_name = 'mk_seq_preln_d1_jaxref_r4_71a233'

def setup_inputs(seed: int=0):
    np.random.seed(seed)
    _w = jnp.asarray

    def _L0_attn_setup():
        import jax, jax.numpy as jnp
        import numpy as np
        B, L, D = (2, 512, 512)
        DIN, N, R, K = (1024, 16, 128, 4)

        def _mamba_forward(hidden_states, in_proj_w, conv1d_w, x_proj_w, dt_proj_w, dt_proj_bias, A_log, D_param, out_proj_w):
            b, l, _ = hidden_states.shape
            xz = jnp.einsum('bld,ed->ble', hidden_states, in_proj_w)
            x, z = jnp.split(xz, 2, axis=-1)
            xp = jnp.pad(x, ((0, 0), (K - 1, 0), (0, 0)))
            xc = sum((conv1d_w[:, k] * xp[:, k:k + l, :] for k in range(K)))
            xc = jax.nn.silu(xc)
            x_dbl = jnp.einsum('bld,ed->ble', xc, x_proj_w)
            dt_r = x_dbl[..., :R]
            Bc = x_dbl[..., R:R + N]
            Cc = x_dbl[..., R + N:]
            delta = jax.nn.softplus(jnp.einsum('blr,dr->bld', dt_r, dt_proj_w) + dt_proj_bias)
            A = -jnp.exp(A_log)

            def step(h, inp):
                delta_t, B_t, C_t, x_t = inp
                dA = jnp.exp(delta_t[..., None] * A)
                h = h * dA + (delta_t * x_t)[..., None] * B_t[:, None, :]
                y_t = jnp.einsum('bdn,bn->bd', h, C_t)
                return (h, y_t)
            inputs = (jnp.swapaxes(delta, 0, 1), jnp.swapaxes(Bc, 0, 1), jnp.swapaxes(Cc, 0, 1), jnp.swapaxes(xc, 0, 1))
            h0 = jnp.zeros((b, DIN, N), dtype=xc.dtype)
            _, y = jax.lax.scan(step, h0, inputs)
            y = jnp.swapaxes(y, 0, 1)
            y = y + xc * D_param
            y = y * jax.nn.silu(z)
            return jnp.einsum('bld,ed->ble', y, out_proj_w)
        key = jax.random.key(seed)
        ks = jax.random.split(key, 9)
        hidden_states = jax.random.normal(ks[0], (B, L, D), dtype=jnp.float32) * 0.02
        in_proj_w = jax.random.normal(ks[1], (2 * DIN, D), dtype=jnp.float32) * (1.0 / np.sqrt(D))
        conv1d_w = jax.random.normal(ks[2], (DIN, K), dtype=jnp.float32) * (1.0 / np.sqrt(DIN))
        x_proj_w = jax.random.normal(ks[3], (R + 2 * N, DIN), dtype=jnp.float32) * (1.0 / np.sqrt(DIN))
        dt_proj_w = jax.random.normal(ks[4], (DIN, R), dtype=jnp.float32) * (1.0 / np.sqrt(R))
        dt = jnp.exp(jax.random.uniform(ks[5], (DIN,)) * (np.log(0.1) - np.log(0.001)) + np.log(0.001))
        dt = jnp.clip(dt, 0.0001, None)
        dt_proj_bias = dt + jnp.log(-jnp.expm1(-dt))
        A_log = jnp.broadcast_to(jnp.log(jnp.arange(1, N + 1, dtype=jnp.float32)), (DIN, N))
        D_param = jnp.ones((DIN,), dtype=jnp.float32)
        out_proj_w = jax.random.normal(ks[6], (D, DIN), dtype=jnp.float32) * (1.0 / np.sqrt(DIN))
        return {'hidden_states': hidden_states, 'in_proj_w': in_proj_w, 'conv1d_w': conv1d_w, 'x_proj_w': x_proj_w, 'dt_proj_w': dt_proj_w, 'dt_proj_bias': dt_proj_bias, 'A_log': A_log, 'D_param': D_param, 'out_proj_w': out_proj_w}
    _L0_attn_in = _L0_attn_setup()

    def _L0_ffn_setup():
        import jax, jax.numpy as jnp
        import numpy as np
        E = 8
        TOP_K = 2
        D = 512
        M = 1792
        B, S = (2, 512)
        key = jax.random.key(seed)
        kx, kg, k1, k2, k3 = jax.random.split(key, 5)
        x = jax.random.normal(kx, (B, S, D), dtype=jnp.float32)
        gate_w = jax.random.normal(kg, (D, E), dtype=jnp.float32) / np.sqrt(D)
        w1 = jax.random.normal(k1, (E, D, M), dtype=jnp.float32) / np.sqrt(D)
        w2 = jax.random.normal(k2, (E, M, D), dtype=jnp.float32) / np.sqrt(M)
        w3 = jax.random.normal(k3, (E, D, M), dtype=jnp.float32) / np.sqrt(D)
        return {'x': x, 'gate_w': gate_w, 'w1': w1, 'w2': w2, 'w3': w3}
    _L0_ffn_in = _L0_ffn_setup()
    _d = {'L0_attn_hidden_states': _L0_attn_in['hidden_states'], 'L0_attn_in_proj_w': _L0_attn_in['in_proj_w'], 'L0_attn_conv1d_w': _L0_attn_in['conv1d_w'], 'L0_attn_x_proj_w': _L0_attn_in['x_proj_w'], 'L0_attn_dt_proj_w': _L0_attn_in['dt_proj_w'], 'L0_attn_dt_proj_bias': _L0_attn_in['dt_proj_bias'], 'L0_attn_A_log': _L0_attn_in['A_log'], 'L0_attn_D_param': _L0_attn_in['D_param'], 'L0_attn_out_proj_w': _L0_attn_in['out_proj_w'], 'L0_ffn_gate_w': _L0_ffn_in['gate_w'], 'L0_ffn_w1': _L0_ffn_in['w1'], 'L0_ffn_w2': _L0_ffn_in['w2'], 'L0_ffn_w3': _L0_ffn_in['w3']}
    _x0 = _d['L0_attn_hidden_states']
    _d['L0_attn_hidden_states'] = jax.random.normal(jax.random.fold_in(jax.random.key(seed), 1), (8, 512, 512), dtype=_x0.dtype)
    del _x0
    return _d

def reference(L0_attn_hidden_states, L0_attn_in_proj_w, L0_attn_conv1d_w, L0_attn_x_proj_w, L0_attn_dt_proj_w, L0_attn_dt_proj_bias, L0_attn_A_log, L0_attn_D_param, L0_attn_out_proj_w, L0_ffn_gate_w, L0_ffn_w1, L0_ffn_w2, L0_ffn_w3):

    def _L0_attn_ref(hidden_states, in_proj_w, conv1d_w, x_proj_w, dt_proj_w, dt_proj_bias, A_log, D_param, out_proj_w):
        import jax, jax.numpy as jnp
        import numpy as np
        B, L, D = (2, 512, 512)
        DIN, N, R, K = (1024, 16, 128, 4)

        def _mamba_forward(hidden_states, in_proj_w, conv1d_w, x_proj_w, dt_proj_w, dt_proj_bias, A_log, D_param, out_proj_w):
            b, l, _ = hidden_states.shape
            xz = jnp.einsum('bld,ed->ble', hidden_states, in_proj_w)
            x, z = jnp.split(xz, 2, axis=-1)
            xp = jnp.pad(x, ((0, 0), (K - 1, 0), (0, 0)))
            xc = sum((conv1d_w[:, k] * xp[:, k:k + l, :] for k in range(K)))
            xc = jax.nn.silu(xc)
            x_dbl = jnp.einsum('bld,ed->ble', xc, x_proj_w)
            dt_r = x_dbl[..., :R]
            Bc = x_dbl[..., R:R + N]
            Cc = x_dbl[..., R + N:]
            delta = jax.nn.softplus(jnp.einsum('blr,dr->bld', dt_r, dt_proj_w) + dt_proj_bias)
            A = -jnp.exp(A_log)

            def step(h, inp):
                delta_t, B_t, C_t, x_t = inp
                dA = jnp.exp(delta_t[..., None] * A)
                h = h * dA + (delta_t * x_t)[..., None] * B_t[:, None, :]
                y_t = jnp.einsum('bdn,bn->bd', h, C_t)
                return (h, y_t)
            inputs = (jnp.swapaxes(delta, 0, 1), jnp.swapaxes(Bc, 0, 1), jnp.swapaxes(Cc, 0, 1), jnp.swapaxes(xc, 0, 1))
            h0 = jnp.zeros((b, DIN, N), dtype=xc.dtype)
            _, y = jax.lax.scan(step, h0, inputs)
            y = jnp.swapaxes(y, 0, 1)
            y = y + xc * D_param
            y = y * jax.nn.silu(z)
            return jnp.einsum('bld,ed->ble', y, out_proj_w)
        return _mamba_forward(hidden_states, in_proj_w, conv1d_w, x_proj_w, dt_proj_w, dt_proj_bias, A_log, D_param, out_proj_w)

    def _L0_ffn_ref(x, gate_w, w1, w2, w3):
        import jax, jax.numpy as jnp
        import numpy as np
        E = 8
        TOP_K = 2
        D = 512
        M = 1792
        B, S = (2, 512)
        b, s, d = x.shape
        x_flat = x.reshape(-1, d)
        router_logits = x_flat @ gate_w
        router_probs = jax.nn.softmax(router_logits, axis=-1)
        topk_w, topk_idx = jax.lax.top_k(router_probs, TOP_K)
        topk_w = topk_w / jnp.sum(topk_w, axis=-1, keepdims=True)
        idx_flat = topk_idx.reshape(-1)
        sort_idx = jnp.argsort(idx_flat)
        x_rep_sort = jnp.take(x_flat, sort_idx // TOP_K, axis=0)
        group_sizes = jnp.bincount(idx_flat, length=E).astype(jnp.int32)
        h = jax.lax.ragged_dot(x_rep_sort, w1, group_sizes)
        h = jax.nn.silu(h) * jax.lax.ragged_dot(x_rep_sort, w3, group_sizes)
        out_sort = jax.lax.ragged_dot(h, w2, group_sizes)
        inv_sort_idx = jnp.argsort(sort_idx)
        out_rep = jnp.take(out_sort, inv_sort_idx, axis=0).reshape(-1, TOP_K, d)
        out = jnp.einsum('tkd,tk->td', out_rep, topk_w)
        return out.reshape(b, s, d)
    x = L0_attn_hidden_states
    x = x + _L0_attn_ref(_layernorm(x, axis=-1), L0_attn_in_proj_w, L0_attn_conv1d_w, L0_attn_x_proj_w, L0_attn_dt_proj_w, L0_attn_dt_proj_bias, L0_attn_A_log, L0_attn_D_param, L0_attn_out_proj_w)
    x = x + _L0_ffn_ref(_layernorm(x, axis=-1), L0_ffn_gate_w, L0_ffn_w1, L0_ffn_w2, L0_ffn_w3)
    return x

_drawn_inputs = setup_inputs


def setup_inputs(seed=0):
    import zlib

    import numpy as np

    out = dict(_drawn_inputs(seed))
    spreads = {'L0_attn_D_param': (1.0, 0.6)}
    factors = {'L0_attn_x_proj_w': 8.0,
     'L0_attn_dt_proj_w': 8.0,
     'L0_attn_dt_proj_bias': 8.0,
     'L0_attn_A_log': 8.0}
    for name, (base, spread) in spreads.items():
        noise = np.random.default_rng([zlib.crc32(name.encode()), seed]).standard_normal(out[name].shape)
        drawn = base * np.exp(spread * noise) if base else spread * noise
        out[name] = jnp.asarray(drawn.astype(out[name].dtype))
    for name, factor in factors.items():
        out[name] = (out[name] * factor).astype(out[name].dtype)
    return out
```

```python
from contextlib import ExitStack

import numpy as np

import concourse.bass as bass
from concourse import mybir

F32 = mybir.dt.float32
I32 = mybir.dt.int32
ALU = mybir.AluOpType
ACT = mybir.ActivationFunctionType
AXX = mybir.AxisListType.X

P = 128
B, L, D = 8, 512, 512
DIN, N, R, K = 1024, 16, 128, 4
E, M = 8, 1792
EPS = 1e-5

TT = L // P
DC = D // P
CH = DIN // P
UN = 4
UPC = N // UN
UL = UN * L
QL = 2 * L

TOKENS = B * L
REGION = TOKENS + P
RW = D + 2
TOKCOL, WCOL = D, D + 1
DUMMY = E * REGION
NT = 2 * TOKENS // P + E - 1
PADTOK = TOKENS

WCH = [(0, 512), (512, 512), (1024, 512), (1536, 256)]
NQ = len(WCH)
MK = M // P
LN1P_SMALL = 1.0 / 128


def mixer(nc, x, w_in, conv_w, w_x, w_dt, dt_bias, a_log, d_par, w_out, gate, out, rows_d, bc_d, cnt_d):
    with ExitStack() as ctx:
        sb = lambda name, shape, dt=F32: ctx.enter_context(nc.sbuf_tensor(name, shape, dt))
        pb = lambda name, shape: ctx.enter_context(nc.psum_tensor(name, shape, F32))
        sem = lambda name: ctx.enter_context(nc.semaphore(name))

        wx = sb("wx", [P, CH, R + 2 * N])
        wdt = sb("wdt", [P, DIN])
        wout = sb("wout", [P, CH, D])
        wgate = sb("wgate", [P, DC, E])
        convw = sb("convw", [P, CH, K])
        dtb = sb("dtb", [P, CH])
        dpar = sb("dpar", [P, CH])
        aneg = sb("aneg", [P, CH, N])
        ident = sb("ident", [P, P])
        before = sb("before", [P, P])
        ones = sb("ones", [P, P])
        iota_e = sb("iota_e", [P, TT, E])
        iota_e8 = sb("iota_e8", [P, TT, E])
        ebase = sb("ebase", [P, E])
        tok = sb("tok", [P, TT])

        xt = sb("xt", [P, TT, D])
        rows = [sb(f"rows{k}", [P, TT, RW]) for k in range(2)]
        xc = sb("xc", [P, CH, L])
        sz = sb("sz", [P, CH, L])
        delta = sb("delta", [P, CH, L])
        bc = sb("bc", [P, 2 * N, L])
        xnT = bc[:, 0:DC, :]
        wk = sb("wk", [P, 4 * UL])
        win = wk[:, :].rearrange("p (d e) -> p d e", d=DC)
        usp = wk[:, 0:CH * L]
        rsp = wk[:, CH * L:2 * CH * L]
        dA = [wk[:, s * UL:(s + 1) * UL].rearrange("p (n t) -> p n t", n=UN) for s in range(2)]
        hs = [wk[:, (2 + s) * UL:(3 + s) * UL].rearrange("p (n t) -> p n t", n=UN) for s in range(2)]
        tsp = sb("tsp", [P, QL])
        dtr = sb("dtr", [P, L])
        bcs = sb("bcs", [2 * N, L])
        dx = tsp[:, 0:L]
        ytmp = tsp[:, L:2 * L]
        st = sb("st", [P, TT, 6])
        mv = sb("mv", [P, TT, 2])
        ve = sb("ve", [P, TT])
        sd = sb("sd", [P, TT])
        rs = sb("rs", [P, TT])
        nt = sb("nt", [P, TT])
        lg = sb("lg", [P, TT, E])
        lg2 = sb("lg2", [P, TT, E])
        le = sb("le", [P, TT, E])
        oh = [sb(f"oh{k}", [P, TT, E]) for k in range(2)]
        sel = sb("sel", [P, TT, E])
        pos = sb("pos", [P, TT, E])
        r1 = sb("r1", [P, TT])
        pk = [sb(f"pk{k}", [P, TT]) for k in range(2)]
        posk = [sb(f"posk{k}", [P, TT]) for k in range(2)]
        idx = [sb(f"idx{k}", [P, TT], I32) for k in range(2)]

        pT = [pb(f"pT{s}", [P, DC, P]) for s in range(2)]
        pM = [pb(f"pM{s}", [P, 512]) for s in range(2)]
        pY = [pb(f"pY{s}", [P, L]) for s in range(2)]
        pR = pb("pR", [P, 2, TT + 1, E])

        consts_in = sem("consts_in")
        consts_set = sem("consts_set")
        a_exp = sem("a_exp")
        a_neg = sem("a_neg")
        x_in = sem("x_in")
        win_in = sem("win_in")
        bc_stored = sem("bc_stored")
        b_in = sem("b_in")
        c_in = sem("c_in")
        x1_stored = sem("x1_stored")
        cnt_stored = sem("cnt_stored")
        step = sem("step")
        var_ready = sem("var_ready")
        sd_ready = sem("sd_ready")
        xn_ready = sem("xn_ready")
        turned = sem("turned")
        tcopied = sem("tcopied")
        xz_mm = sem("xz_mm")
        tap3 = sem("tap3")
        conv_step = sem("conv_step")
        xc_ready = sem("xc_ready")
        z_ready = sem("z_ready")
        xp_mm = sem("xp_mm")
        xp_copied = sem("xp_copied")
        dt_mm = sem("dt_mm")
        dt_read = sem("dt_read")
        ln1p = sem("ln1p")
        delta_ready = sem("delta_ready")
        dx_ready = sem("dx_ready")
        decay = sem("decay")
        zeroed = sem("zeroed")
        inflow = sem("inflow")
        scanned = sem("scanned")
        weighed = sem("weighed")
        summed = sem("summed")
        ysum_read = [sem(f"ysum_read{j}") for j in range(2)]
        gated = sem("gated")
        out_mm = sem("out_mm")
        x1_ready = sem("x1_ready")
        logits_mm = sem("logits_mm")
        exp_in = sem("exp_in")
        exp_out = sem("exp_out")
        sel_ready = sem("sel_ready")
        rank_mm = sem("rank_mm")
        rows_ready = sem("rows_ready")
        scattered = sem("scattered")
        turn = sem("turn")
        sp_turn = sem("sp_turn")
        dve_turn = sem("dve_turn")

        NCONST = 9
        STEPS = 65

        block = ctx.enter_context(nc.Block())

        @block.sync
        def _(sp):
            for dst, src in ((wx, w_x), (wdt, w_dt), (wout, w_out), (wgate, gate), (convw, conv_w),
                             (dtb, dt_bias), (dpar, d_par), (aneg, a_log)):
                sp.dma_start(dst[tuple([slice(None)] * len(dst.shape))], src).then_inc(consts_in, 16)
            sp.wait_ge(consts_set, 1)
            sp.dma_start(out[TOKENS:TOKENS + P, :], ytmp).then_inc(consts_in, 16)
            with sp.Fori(0, B) as b:
                sp.wait_ge(xn_ready, 2 * TT * b)
                sp.sem_inc(sp_turn, 1)
                sp.wait_ge(x1_stored, 16 * b)
                sp.dma_start(xt[:, :, :], x[bass.ds(b * L, L), :].rearrange("(t p) d -> p t d", p=P))\
                  .then_inc(x_in, 16)
                sp.wait_ge(gated, CH * b)
                sp.dma_start(win, w_in).then_inc(win_in, 16)
                sp.wait_ge(xp_copied, 2 * b + 2)
                sp.dma_start(bc_d, bcs[:, :]).then_inc(bc_stored, 16)
                sp.wait_ge(bc_stored, 16 * b + 16)
                sp.dma_start(bc[:, 0:N, :], bc_d[0:N, :].rearrange("(a n) t -> a n t", a=1).to_broadcast([P, N, L]))\
                  .then_inc(b_in, 16)
                sp.dma_start(bc[:, N:2 * N, :], bc_d[N:2 * N, :].rearrange("(a n) t -> a n t", a=1).to_broadcast([P, N, L]))\
                  .then_inc(c_in, 16)
                sp.wait_ge(x1_ready, TT * b + TT)
                sp.dma_start(out[bass.ds(b * L, L), :].rearrange("(t p) d -> p t d", p=P), xt[:, :, :])\
                  .then_inc(x1_stored, 16)
            sp.wait_ge(step, STEPS * B)
            sp.dma_start(cnt_d, ebase[0:1, :]).then_inc(cnt_stored, 16)
            sp.wait_ge(cnt_stored, 16)
            sp.wait_ge(x1_stored, 16 * B)
            sp.wait_ge(consts_in, 16 * NCONST)

        @block.gpsimd
        def _(pool):
            pool.memset(ytmp, 0.0).then_inc(consts_set, 1)
            pool.memset(ident[:, :], 0.0).then_inc(consts_set, 1)
            pool.memset(ones[:, :], 1.0).then_inc(consts_set, 1)
            pool.wait_ge(consts_set, 3)
            pool.affine_select(out=ident[:, :], in_=ident[:, :], compare_op=ALU.not_equal, fill=1.0, base=0,
                               pattern=[[-1, P]], channel_multiplier=1).then_inc(consts_set, 1)
            pool.affine_select(out=before[:, :], in_=ones[:, :], compare_op=ALU.is_gt, fill=0.0, base=0,
                               pattern=[[1, P]], channel_multiplier=-1).then_inc(consts_set, 1)
            pool.iota(iota_e[:, :, :], pattern=[[0, TT], [1, E]], base=0, channel_multiplier=0,
                      allow_small_or_imprecise_dtypes=True).then_inc(consts_set, 1)
            pool.iota(iota_e8[:, :, :], pattern=[[0, TT], [1, E]], base=E, channel_multiplier=0,
                      allow_small_or_imprecise_dtypes=True).then_inc(consts_set, 1)
            pool.iota(ebase[:, :], pattern=[[REGION, E]], base=0, channel_multiplier=0,
                      allow_small_or_imprecise_dtypes=True).then_inc(consts_set, 1)
            pool.iota(tok[:, :], pattern=[[P, TT]], base=0, channel_multiplier=1,
                      allow_small_or_imprecise_dtypes=True).then_inc(consts_set, 1)
            with pool.Fori(0, B) as b:
                pool.wait_ge(rows_ready, b + 1)
                pool.sem_inc(turn, 1)
                for k in range(2):
                    for t in range(TT):
                        pool.indirect_dma_start(
                            out=rows_d, out_offset=bass.IndirectOffsetOnAxis(ap=idx[k][:, t:t + 1], axis=0),
                            in_=rows[k][:, t, :], in_offset=None).then_inc(scattered, 16)
            pool.wait_ge(scattered, 16 * 2 * TT * B)

        @block.scalar
        def _(act):
            act.wait_ge(consts_in, 16 * NCONST)
            act.activation(aneg[:, :, :], aneg[:, :, :], ACT.Exp).then_inc(a_exp, 1)
            act.wait_ge(a_neg, 1)

            def copy_turned(b, i):
                act.wait_ge(turned, 2 * TT * b + i + 1)
                t = i % TT
                act.activation(xnT[:, :, t * P:(t + 1) * P], pT[i % 2][:, :, :], ACT.Copy).then_inc(tcopied, 1)

            with act.Fori(0, B) as b:
                act.wait_ge(var_ready, 2 * b + 1)
                act.activation(sd[:, :], ve[:, :], ACT.Sqrt).then_inc(sd_ready, 1)
                for i in range(TT):
                    copy_turned(b, i)
                act.wait_ge(gated, CH * b)
                for c in range(CH + 1):
                    if c < CH:
                        act.wait_ge(xz_mm, 2 * CH * b + c + 1)
                        act.activation(xc[:, c, :], pM[c % 2][:, :], ACT.Copy, scale=convw[:, c, K - 1:K])\
                           .then_inc(tap3, 1)
                    if c >= 1:
                        act.wait_ge(conv_step, (K - 1) * (CH * b + c))
                        act.activation(xc[:, c - 1, :], xc[:, c - 1, :], ACT.Silu).then_inc(xc_ready, 1)
                for c in range(CH):
                    act.wait_ge(xz_mm, 2 * CH * b + CH + c + 1)
                    act.activation(sz[:, c, :], pM[c % 2][:, :], ACT.Silu).then_inc(z_ready, 1)
                act.wait_ge(xp_mm, 2 * b + 1)
                act.activation(bcs[:, :], pM[0][0:2 * N, :], ACT.Copy).then_inc(xp_copied, 1)
                act.wait_ge(xp_mm, 2 * b + 2)
                act.activation(dtr[:, :], pM[1][:, :], ACT.Copy).then_inc(xp_copied, 1)
                for c in range(CH):
                    act.wait_ge(dt_mm, CH * b + c + 1)
                    act.activation(usp[:, c * L:(c + 1) * L], pM[c % 2][:, :], ACT.Abs, bias=dtb[:, c:c + 1])
                    act.activation(rsp[:, c * L:(c + 1) * L], pM[c % 2][:, :], ACT.Relu, bias=dtb[:, c:c + 1])\
                       .then_inc(dt_read, 1)
                act.wait_ge(dt_read, CH * b + CH)
                act.activation(usp, usp, ACT.Exp, scale=-1.0).then_inc(ln1p, 1)
                act.wait_ge(ln1p, 2 * b + 1)
                act.activation(delta[:, :, :].rearrange("p c t -> p (c t)"), usp, ACT.Ln, bias=ones[:, 0:1])\
                   .then_inc(ln1p, 1)
                act.wait_ge(delta_ready, b + 1)
                with act.Fori(0, CH) as c:
                    for u in range(UPC):
                        if u >= 2:
                            act.wait_ge(summed, (CH * b + c) * UPC + u - 1)
                        else:
                            act.wait_ge(summed, (CH * b + c) * UPC)
                        for i in range(UN):
                            e = act.activation(dA[u % 2][:, i, 1:L], delta[:, bass.ds(c, 1), 1:L].rearrange("p c t -> p (c t)"),
                                               ACT.Exp, scale=aneg[:, bass.ds(c, 1), u * UN + i:u * UN + i + 1].rearrange("p c n -> p (c n)"))
                        e.then_inc(decay, 1)
                act.wait_ge(var_ready, 2 * b + 2)
                act.activation(sd[:, :], ve[:, :], ACT.Sqrt).then_inc(sd_ready, 1)
                for i in range(TT, 2 * TT):
                    copy_turned(b, i)
                act.wait_ge(exp_in, b + 1)
                act.activation(le[:, :, :], le[:, :, :], ACT.Exp).then_inc(exp_out, 1)

        @block.tensor
        def _(pe):
            pe.wait_ge(consts_in, 16 * NCONST)
            pe.wait_ge(consts_set, 9)

            def turn_rows(b, i):
                pe.wait_ge(tcopied, 2 * TT * b + max(i - 1, 0))
                for d in range(DC):
                    m = pe.transpose(pT[i % 2][:, d, :], rows[0][:, i % TT, d * P:(d + 1) * P], ident[:, :])
                m.then_inc(turned, 1)

            with pe.Fori(0, B) as b:
                for t in range(TT):
                    pe.wait_ge(xn_ready, 2 * TT * b + t + 1)
                    turn_rows(b, t)
                pe.wait_ge(tcopied, 2 * TT * b + TT)
                pe.wait_ge(win_in, 16 * b + 16)
                pe.wait_ge(x1_ready, TT * b)
                for c in range(2 * CH):
                    if 2 <= c < CH + 2:
                        pe.wait_ge(conv_step, (K - 1) * (CH * b + c - 1))
                    if c >= CH + 2:
                        pe.wait_ge(z_ready, CH * b + c - CH - 1)
                    for d in range(DC):
                        m = pe.matmul(pM[c % 2][:, :], win[:, d, c * P:(c + 1) * P], xnT[:, d, :],
                                      start=d == 0, stop=d == DC - 1)
                    m.then_inc(xz_mm, 1)
                pe.wait_ge(xc_ready, CH * b + CH)
                pe.wait_ge(z_ready, CH * b + CH)
                for c in range(CH):
                    m = pe.matmul(pM[0][0:2 * N, :], wx[:, c, R:R + 2 * N], xc[:, c, :], start=c == 0, stop=c == CH - 1)
                m.then_inc(xp_mm, 1)
                for c in range(CH):
                    m = pe.matmul(pM[1][:, :], wx[:, c, 0:R], xc[:, c, :], start=c == 0, stop=c == CH - 1)
                m.then_inc(xp_mm, 1)
                pe.wait_ge(xp_copied, 2 * b + 2)
                for c in range(CH):
                    if c >= 2:
                        pe.wait_ge(dt_read, CH * b + c - 1)
                    pe.matmul(pM[c % 2][:, :], wdt[:, c * P:(c + 1) * P], dtr[:, :], start=True, stop=True)\
                      .then_inc(dt_mm, 1)
                with pe.Fori(0, CH // 2) as c2:
                    for j in range(2):
                        chunk = CH * b + 2 * c2 + j
                        pe.wait_ge(ysum_read[j], CH // 2 * b + c2)
                        for u in range(UPC):
                            pe.wait_ge(weighed, chunk * UPC + u + 1)
                            for i in range(UN):
                                m = pe.matmul(pY[j][:, :], ident[:, :], dA[u % 2][:, i, :],
                                              start=u == 0 and i == 0, stop=u == UPC - 1 and i == UN - 1)
                            m.then_inc(summed, 1)
                pe.wait_ge(gated, CH * b + CH)
                for t in range(TT):
                    if t >= 2:
                        pe.wait_ge(x1_ready, TT * b + t - 1)
                    else:
                        pe.wait_ge(dt_read, CH * b + CH)
                    for c in range(CH):
                        m = pe.matmul(pM[t % 2][:, :], sz[:, c, t * P:(t + 1) * P], wout[:, c, :],
                                      start=c == 0, stop=c == CH - 1)
                    m.then_inc(out_mm, 1)
                for t in range(TT):
                    pe.wait_ge(xn_ready, 2 * TT * b + TT + t + 1)
                    turn_rows(b, TT + t)
                pe.wait_ge(tcopied, 2 * TT * b + 2 * TT)
                pe.wait_ge(rows_ready, b)
                for t in range(TT):
                    for d in range(DC):
                        m = pe.matmul(pR[:, 0, t, :], xnT[:, d, t * P:(t + 1) * P], wgate[:, d, :],
                                      start=d == 0, stop=d == DC - 1)
                m.then_inc(logits_mm, 1)
                pe.wait_ge(sel_ready, b + 1)
                for t in range(TT + 1):
                    for s in range(min(t + 1, TT)):
                        m = pe.matmul(pR[:, 1, t, :], before[:, :] if s == t else ones[:, :], sel[:, s, :],
                                      start=s == 0, stop=s == min(t, TT - 1))
                m.then_inc(rank_mm, 1)

        @block.vector
        def _(dve):
            dve.wait_ge(a_exp, 1)
            dve.wait_ge(consts_set, 9)
            dve.tensor_scalar(aneg[:, :, :], aneg[:, :, :], -1.0, None, ALU.mult).then_inc(a_neg, 1)

            with dve.Fori(0, B) as b:
                count = [0]

                def link(ins):
                    count[0] += 1
                    ins.then_inc(step, 1)
                    dve.wait_ge(step, STEPS * b + count[0])

                def norm(half):
                    for t in range(TT):
                        if half:
                            dve.wait_ge(out_mm, TT * b + t + 1)
                            dve.tensor_tensor(xt[:, t, :], pM[t % 2][:, :], xt[:, t, :], ALU.add).then_inc(x1_ready, 1)
                            dve.wait_ge(x1_ready, TT * b + t + 1)
                        i = dve.bn_stats(st[:, t, :], xt[:, t, :])
                    link(i)
                    dve.sem_inc(dve_turn, 1)
                    for t in range(TT):
                        i = dve.bn_aggr(mv[:, t, :], st[:, t, :])
                    link(i)
                    dve.tensor_scalar(ve[:, :], mv[:, :, 1], EPS, None, ALU.add).then_inc(var_ready, 1)
                    dve.wait_ge(sd_ready, 2 * b + half + 1)
                    link(dve.reciprocal(rs[:, :], sd[:, :]))
                    link(dve.tensor_tensor(nt[:, :], rs[:, :], rs[:, :], ALU.mult))
                    link(dve.tensor_tensor(nt[:, :], nt[:, :], ve[:, :], ALU.mult))
                    link(dve.tensor_scalar(nt[:, :], nt[:, :], -0.5, 1.5, ALU.mult, ALU.add))
                    link(dve.tensor_tensor(rs[:, :], rs[:, :], nt[:, :], ALU.mult))
                    for t in range(TT):
                        if half:
                            dve.tensor_scalar(rows[1][:, t, 0:D], xt[:, t, :], mv[:, t, 0:1], rs[:, t:t + 1],
                                              ALU.subtract, ALU.mult)
                        dve.tensor_scalar(rows[0][:, t, 0:D], xt[:, t, :], mv[:, t, 0:1], rs[:, t:t + 1],
                                          ALU.subtract, ALU.mult).then_inc(xn_ready, 1)

                dve.wait_ge(x_in, 16 * b + 16)
                dve.wait_ge(scattered, 16 * 2 * TT * b)
                norm(0)
                for c in range(CH):
                    dve.wait_ge(tap3, CH * b + c + 1)
                    for k in range(K - 1):
                        s = K - 1 - k
                        if k:
                            dve.wait_ge(conv_step, (K - 1) * (CH * b + c) + k)
                        dve.scalar_tensor_tensor(xc[:, c, s:L], pM[c % 2][:, 0:L - s], convw[:, c, k:k + 1],
                                                 xc[:, c, s:L], ALU.mult, ALU.add).then_inc(conv_step, 1)
                dve.wait_ge(ln1p, 2 * b + 2)
                dflat = delta[:, :, :].rearrange("p c t -> p (c t)")
                for j in range(CH // 2):
                    part = slice(j * QL, (j + 1) * QL)
                    link(dve.tensor_scalar(tsp[:, :], usp[:, part], 1.0 / 3, -0.5, ALU.mult, ALU.add))
                    link(dve.tensor_tensor(tsp[:, :], tsp[:, :], usp[:, part], ALU.mult))
                    link(dve.scalar_tensor_tensor(tsp[:, :], tsp[:, :], 1.0, usp[:, part], ALU.add, ALU.mult))
                    link(dve.tensor_scalar(usp[:, part].bitcast(I32), usp[:, part], LN1P_SMALL, None, ALU.is_lt))
                    dve.sem_inc(dve_turn, 1)
                    link(dve.copy_predicated(dflat[:, part], usp[:, part].bitcast(I32), tsp[:, :]))
                    link(dve.tensor_tensor(dflat[:, part], dflat[:, part], rsp[:, part], ALU.add))
                dve.nop().then_inc(delta_ready, 1)

                dve.wait_ge(b_in, 16 * b + 16)
                dve.wait_ge(c_in, 16 * b + 16)

                def row(buf, c, j):
                    return buf[:, bass.ds(2 * c + j, 1), :].rearrange("p c t -> p (c t)")

                def chunk(c2, j, finish):
                    k0 = (CH * b + 2 * c2 + j) * UPC
                    dve.tensor_tensor(dx, row(delta, c2, j), row(xc, c2, j), ALU.mult).then_inc(dx_ready, 1)
                    dve.wait_ge(dx_ready, CH * b + 2 * c2 + j + 1)
                    dxb = dx.rearrange("p (a t) -> p a t", a=1).to_broadcast([P, UN, L])

                    def feed(u):
                        dve.wait_ge(weighed, k0 + max(u - 1, 0))
                        dve.tensor_tensor(hs[u % 2], dxb, bc[:, u * UN:(u + 1) * UN, :], ALU.mult).then_inc(inflow, 1)

                    feed(0)
                    for u in range(UPC):
                        dve.wait_ge(decay, k0 + u + 1)
                        dve.memset(dA[u % 2][:, :, 0:1], 0.0).then_inc(zeroed, 1)
                        if u + 1 < UPC:
                            feed(u + 1)
                        dve.wait_ge(zeroed, k0 + u + 1)
                        dve.wait_ge(inflow, k0 + u + 1)
                        flat = hs[u % 2].rearrange("p n t -> p (n t)")
                        dve.tensor_tensor_scan(flat, dA[u % 2].rearrange("p n t -> p (n t)"), flat, 0.0,
                                               ALU.mult, ALU.add).then_inc(scanned, 1)
                        if u == 1 and finish:
                            finish_chunk(c2 if j else c2 - 1, 1 - j)
                        dve.wait_ge(scanned, k0 + u + 1)
                        dve.tensor_tensor(dA[u % 2], hs[u % 2], bc[:, N + u * UN:N + (u + 1) * UN, :], ALU.mult)\
                           .then_inc(weighed, 1)

                def finish_chunk(c2, j):
                    n = CH * b + 2 * c2 + j
                    dve.wait_ge(summed, (n + 1) * UPC)
                    dve.scalar_tensor_tensor(ytmp, row(xc, c2, j), dpar[:, bass.ds(2 * c2 + j, 1)], pY[j][:, :],
                                             ALU.mult, ALU.add).then_inc(ysum_read[j], 1)
                    dve.wait_ge(ysum_read[j], CH // 2 * b + c2 + 1)
                    dve.tensor_tensor(row(sz, c2, j), ytmp, row(sz, c2, j), ALU.mult).then_inc(gated, 1)

                chunk(0, 0, False)
                chunk(0, 1, True)
                with dve.Fori(1, CH // 2) as c2:
                    chunk(c2, 0, True)
                    chunk(c2, 1, True)
                finish_chunk(CH // 2 - 1, 1)

                norm(1)
                dve.wait_ge(logits_mm, b + 1)
                link(dve.tensor_copy(lg[:, :, :], pR[:, 0, 0:TT, :]))
                spread = lambda v: v[:, :].rearrange("p (t a) -> p t a", a=1).to_broadcast([P, TT, E])
                src = lg
                for k in range(2):
                    link(dve.tensor_reduce(r1[:, :], src[:, :, :], AXX, ALU.max))
                    if k == 0:
                        dve.tensor_tensor(le[:, :, :], lg[:, :, :], spread(r1), ALU.subtract).then_inc(exp_in, 1)
                    link(dve.tensor_tensor(oh[k][:, :, :], src[:, :, :], spread(r1), ALU.is_equal))
                    link(dve.scalar_tensor_tensor(oh[k][:, :, :], oh[k][:, :, :], -float(E), iota_e8[:, :, :], ALU.mult, ALU.add))
                    link(dve.tensor_reduce(r1[:, :], oh[k][:, :, :], AXX, ALU.min))
                    link(dve.tensor_tensor(oh[k][:, :, :], iota_e[:, :, :], spread(r1), ALU.is_equal))
                    if k == 0:
                        link(dve.scalar_tensor_tensor(lg2[:, :, :], oh[0][:, :, :], -3.0e38, lg[:, :, :], ALU.mult, ALU.add))
                        src = lg2
                dve.tensor_tensor(sel[:, :, :], oh[0][:, :, :], oh[1][:, :, :], ALU.add).then_inc(sel_ready, 1)
                dve.wait_ge(exp_out, b + 1)
                link(dve.tensor_reduce(r1[:, :], le[:, :, :], AXX, ALU.add))
                link(dve.reciprocal(nt[:, :], r1[:, :]))
                link(dve.tensor_tensor(le[:, :, :], le[:, :, :], spread(nt), ALU.mult))
                for k in range(2):
                    link(dve.tensor_tensor(lg2[:, :, :], le[:, :, :], oh[k][:, :, :], ALU.mult))
                    link(dve.tensor_reduce(pk[k][:, :], lg2[:, :, :], AXX, ALU.add))
                link(dve.tensor_tensor(r1[:, :], pk[0][:, :], pk[1][:, :], ALU.add))
                link(dve.reciprocal(r1[:, :], r1[:, :]))
                for k in range(2):
                    dve.tensor_tensor(rows[k][:, :, WCOL], pk[k][:, :], r1[:, :], ALU.mult)
                    dve.tensor_copy(rows[k][:, :, TOKCOL], tok[:, :])
                dve.wait_ge(rank_mm, b + 1)
                base = ebase[:, :].rearrange("p (a e) -> p a e", a=1).to_broadcast([P, TT, E])
                link(dve.tensor_tensor(pos[:, :, :], pR[:, 1, 0:TT, :], base, ALU.add))
                for k in range(2):
                    link(dve.tensor_tensor(lg2[:, :, :], pos[:, :, :], oh[k][:, :, :], ALU.mult))
                    link(dve.tensor_reduce(posk[k][:, :], lg2[:, :, :], AXX, ALU.add))
                    i = dve.tensor_copy(idx[k][:, :], posk[k][:, :])
                i.then_inc(rows_ready, 1)
                dve.tensor_scalar(tok[:, :], tok[:, :], float(L), None, ALU.add)
                link(dve.tensor_tensor(ebase[:, :], ebase[:, :], pR[:, 1, TT, :], ALU.add))
                assert count[0] == STEPS, count[0]


def experts(nc, w1, w2, w3, out, rows_d, cnt_d):
    with ExitStack() as ctx:
        sb = lambda name, shape, dt=F32: ctx.enter_context(nc.sbuf_tensor(name, shape, dt))
        pb = lambda name, shape: ctx.enter_context(nc.psum_tensor(name, shape, F32))
        sem = lambda name: ctx.enter_context(nc.semaphore(name))

        w1s = sb("w1s", [P, DC, M])
        w3s = sb("w3s", [P, DC, M])
        w2s = sb("w2s", [P, MK, D])
        ident = sb("ident2", [P, P])
        xr = sb("xr", [P, RW])
        xT = sb("xT", [P, DC, P])
        gate = [sb(f"gate{s}", [P, 512]) for s in range(2)]
        hh = sb("hh", [P, M])
        hT = sb("hT", [P, MK, P])
        wrow = sb("wrow", [P, 1])
        trow = sb("trow", [P, 1], I32)
        ow = sb("ow", [P, D])
        pad = sb("pad", [P, RW])
        ptok = sb("ptok", [P, 1])
        ends = sb("ends", [1, E])
        cnt = sb("cnt", [1, E])
        ci = sb("ci", [1, E], I32)
        tiles = sb("tiles", [1, E])
        ebase = sb("ebase2", [1, E])
        tnum = sb("tnum", [1, NT, E])
        over = sb("over", [1, NT, E])
        ex = sb("ex", [1, NT])
        used = sb("used", [1, NT])
        tn = sb("tn", [1, NT])
        first = sb("first", [1, NT])
        one8 = sb("one8", [1, E])
        row_i = sb("row_i", [1, NT], I32)
        ex_i = sb("ex_i", [1, NT], I32)
        load_i = sb("load_i", [1, NT], I32)
        pad_i = sb("pad_i", [1, E + 1], I32)

        pA = [pb(f"pA{s}", [P, 512]) for s in range(2)]
        pB = [pb(f"pB{s}", [P, 512]) for s in range(2)]
        pH = [pb(f"pH{s}", [P, 4, P]) for s in range(2)]
        pX = pb("pX", [P, DC, P])
        pO = pb("pO", [P, D])

        cnt_in = sem("cnt_in")
        set_up = sem("set_up")
        plan = sem("plan")
        padded = sem("padded")
        x_in = sem("x_in2")
        w13_in = [sem(f"w13_in{q}") for q in range(NQ)]
        w2_in = [sem(f"w2_in{q}") for q in range(NQ)]
        x_turned = sem("x_turned")
        x_copied = sem("x_copied")
        meta = sem("meta")
        up_mm = sem("up_mm")
        silu = sem("silu")
        h_ready = sem("h_ready")
        h_turned = sem("h_turned")
        h_copied = sem("h_copied")
        down_mm = sem("down_mm")
        ow_ready = sem("ow_ready")
        added = sem("added")
        turn = sem("turn2")

        PLAN = 18
        block = ctx.enter_context(nc.Block())

        @block.gpsimd
        def _(pool):
            pool.memset(ident[:, :], 0.0).then_inc(set_up, 1)
            pool.memset(pad[:, :], 0.0).then_inc(set_up, 1)
            pool.memset(one8[:, :], 1.0).then_inc(set_up, 1)
            pool.wait_ge(set_up, 3)
            pool.affine_select(out=ident[:, :], in_=ident[:, :], compare_op=ALU.not_equal, fill=1.0, base=0,
                               pattern=[[-1, P]], channel_multiplier=1).then_inc(set_up, 1)
            pool.iota(ptok[:, :], pattern=[[0, 1]], base=PADTOK, channel_multiplier=1,
                      allow_small_or_imprecise_dtypes=True).then_inc(set_up, 1)
            pool.iota(tnum[:, :, :], pattern=[[1, NT], [0, E]], base=0, channel_multiplier=0,
                      allow_small_or_imprecise_dtypes=True).then_inc(set_up, 1)
            pool.iota(tn[:, :], pattern=[[1, NT]], base=0, channel_multiplier=0,
                      allow_small_or_imprecise_dtypes=True).then_inc(set_up, 1)
            pool.iota(ebase[:, :], pattern=[[REGION, E]], base=0, channel_multiplier=0,
                      allow_small_or_imprecise_dtypes=True).then_inc(set_up, 1)
            with pool.Fori(0, NT) as t:
                pool.wait_ge(ow_ready, t + 1)
                pool.wait_ge(added, 16 * t)
                pool.sem_inc(turn, 1)
                pool.indirect_dma_start(out=out, out_offset=bass.IndirectOffsetOnAxis(ap=trow[:, 0:1], axis=0),
                                        in_=ow[:, :], in_offset=None, compute_op=ALU.add).then_inc(added, 16)
            pool.wait_ge(added, 16 * NT)

        @block.sync
        def _(sp):
            sp.dma_start(cnt[:, :], cnt_d).then_inc(cnt_in, 16)
            sp.wait_ge(plan, PLAN)
            with sp.Fori(0, E + 1) as e:
                r = sp.value_load(pad_i[0:1, bass.ds(e, 1)], min_val=0, max_val=DUMMY)
                sp.dma_start(rows_d[bass.ds(r, P), :], pad[:, :]).then_inc(padded, 16)
            sp.wait_ge(padded, 16 * (E + 1))

            def load_rows(t):
                r = sp.value_load(row_i[0:1, bass.ds(t, 1)], min_val=0, max_val=DUMMY)
                sp.dma_start(xr[:, :], rows_d[bass.ds(r, P), :]).then_inc(x_in, 16)

            def load_up(q, e, c=None):
                lo, n = WCH[q]
                for ws, w in ((w1s, w1), (w3s, w3)):
                    src = w[bass.ds(e * D, D), lo:lo + n].rearrange("(c p) m -> p c m", p=P)
                    if c is None:
                        sp.dma_start(ws[:, :, lo:lo + n], src).then_inc(w13_in[q], 16)
                    else:
                        sp.dma_start(ws[:, :, lo:lo + n], src, cond=c, bounds_check="skip_entire_dma")\
                          .then_inc(w13_in[q], 16)

            def load_down(q, e, c=None):
                lo, n = WCH[q][0] // P, WCH[q][1] // P
                src = w2[bass.ds(e * M + lo * P, n * P), :].rearrange("(k p) d -> p k d", p=P)
                if c is None:
                    sp.dma_start(w2s[:, lo:lo + n, :], src).then_inc(w2_in[q], 16)
                else:
                    sp.dma_start(w2s[:, lo:lo + n, :], src, cond=c, bounds_check="skip_entire_dma")\
                      .then_inc(w2_in[q], 16)

            load_rows(0)
            e0 = sp.value_load(ex_i[0:1, 0:1], min_val=0, max_val=E - 1)
            for q in range(NQ):
                load_up(q, e0)
            for q in range(NQ):
                load_down(q, e0)
            with sp.Fori(0, NT - 1) as t:
                sp.wait_ge(x_turned, t + 1)
                sp.wait_ge(meta, t + 1)
                load_rows(t + 1)
                e1 = sp.value_load(ex_i[0:1, bass.ds(t + 1, 1)], min_val=0, max_val=E - 1)
                new = sp.value_load(load_i[0:1, bass.ds(t + 1, 1)], min_val=0, max_val=1)
                for q in range(NQ):
                    sp.wait_ge(up_mm, NQ * t + q + 1)
                    load_up(q, e1, new > 0)
                for q in range(NQ):
                    sp.wait_ge(down_mm, NQ * t + q + 1)
                    load_down(q, e1, new > 0)

        @block.scalar
        def _(act):
            def tile(t, last):
                def silu_q(q):
                    n = WCH[q][1]
                    act.wait_ge(up_mm, NQ * t + q + 1)
                    act.wait_ge(h_ready, NQ * t + max(q - 1, 0))
                    act.activation(gate[q % 2][:, 0:n], pA[q % 2][:, 0:n], ACT.Silu).then_inc(silu, 1)

                def copy_q(q):
                    lo, n = WCH[q][0] // P, WCH[q][1] // P
                    act.wait_ge(h_turned, NQ * t + q + 1)
                    act.activation(hT[:, lo:lo + n, :], pH[q % 2][:, 0:n, :], ACT.Copy).then_inc(h_copied, 1)

                silu_q(0)
                for q in range(1, NQ):
                    silu_q(q)
                    copy_q(q - 1)
                if not last:
                    act.wait_ge(x_turned, t + 2)
                    act.activation(xT[:, :, :], pX[:, :, :], ACT.Copy).then_inc(x_copied, 1)
                copy_q(NQ - 1)

            act.wait_ge(x_turned, 1)
            act.activation(xT[:, :, :], pX[:, :, :], ACT.Copy).then_inc(x_copied, 1)
            with act.Fori(0, NT - 1) as t:
                tile(t, False)
            tile(NT - 1, True)

        @block.tensor
        def _(pe):
            def turn_rows(t):
                pe.wait_ge(x_in, 16 * t + 16)
                for d in range(DC):
                    m = pe.transpose(pX[:, d, :], xr[:, d * P:(d + 1) * P], ident[:, :])
                m.then_inc(x_turned, 1)

            def tile(t, last):
                def up(q):
                    lo, n = WCH[q]
                    pe.wait_ge(w13_in[q], 32 * t + 32)
                    pe.wait_ge(h_ready, NQ * t + max(q - 1, 0))
                    for ps, ws in ((pA, w1s), (pB, w3s)):
                        for d in range(DC):
                            m = pe.matmul(ps[q % 2][:, 0:n], xT[:, d, :], ws[:, d, lo:lo + n],
                                          start=d == 0, stop=d == DC - 1)
                    m.then_inc(up_mm, 1)

                def turn_h(q):
                    pe.wait_ge(h_ready, NQ * t + q + 1)
                    pe.wait_ge(h_copied, NQ * t + max(q - 1, 0))
                    lo, n = WCH[q][0] // P, WCH[q][1] // P
                    for k in range(n):
                        m = pe.transpose(pH[q % 2][:, k, :], hh[:, (lo + k) * P:(lo + k + 1) * P], ident[:, :])
                    m.then_inc(h_turned, 1)

                def down(q):
                    lo, n = WCH[q][0] // P, WCH[q][1] // P
                    pe.wait_ge(h_copied, NQ * t + q + 1)
                    pe.wait_ge(w2_in[q], 16 * t + 16)
                    for k in range(lo, lo + n):
                        m = pe.matmul(pO[:, :], hT[:, k, :], w2s[:, k, :], start=k == 0, stop=k == MK - 1)
                    m.then_inc(down_mm, 1)

                pe.wait_ge(x_copied, t + 1)
                up(0)
                for q in range(1, NQ):
                    up(q)
                    turn_h(q - 1)
                if not last:
                    turn_rows(t + 1)
                pe.wait_ge(ow_ready, t)
                for q in range(NQ - 1):
                    down(q)
                turn_h(NQ - 1)
                down(NQ - 1)

            pe.wait_ge(set_up, 8)
            turn_rows(0)
            with pe.Fori(0, NT - 1) as t:
                tile(t, False)
            tile(NT - 1, True)

        @block.vector
        def _(dve):
            count = [0]

            def link(ins):
                count[0] += 1
                ins.then_inc(plan, 1)
                dve.wait_ge(plan, count[0])

            dve.wait_ge(set_up, 8)
            dve.wait_ge(cnt_in, 16)
            link(dve.tensor_copy(pad[:, TOKCOL:TOKCOL + 1], ptok[:, :]))
            link(dve.tensor_copy(pad_i[:, 0:E], cnt[:, :]))
            link(dve.memset(pad_i[:, E:E + 1], DUMMY))
            link(dve.tensor_tensor(ends[:, :], cnt[:, :], ebase[:, :], ALU.subtract))
            link(dve.tensor_scalar(ci[:, :], ends[:, :], float(P - 1), None, ALU.add))
            link(dve.tensor_scalar(ci[:, :], ci[:, :], P.bit_length() - 1, None, ALU.logical_shift_right))
            link(dve.tensor_copy(tiles[:, :], ci[:, :]))
            link(dve.tensor_tensor_scan(ends[:, :], one8[:, :], tiles[:, :], 0.0, ALU.mult, ALU.add))
            wide = lambda v: v[:, :].rearrange("p (a e) -> p a e", a=1).to_broadcast([1, NT, E])
            link(dve.tensor_tensor(over[:, :, :], tnum[:, :, :], wide(ends), ALU.is_ge))
            link(dve.tensor_reduce(ex[:, :], over[:, :, :], AXX, ALU.add))
            link(dve.tensor_tensor(over[:, :, :], over[:, :, :], wide(tiles), ALU.mult))
            link(dve.tensor_reduce(used[:, :], over[:, :, :], AXX, ALU.add))
            link(dve.tensor_tensor(used[:, :], tn[:, :], used[:, :], ALU.subtract))
            link(dve.tensor_scalar(used[:, :], used[:, :], float(P), None, ALU.mult))
            link(dve.scalar_tensor_tensor(used[:, :], ex[:, :], float(REGION), used[:, :], ALU.mult, ALU.add))
            dve.tensor_scalar(row_i[:, :], used[:, :], float(DUMMY), None, ALU.min)
            link(dve.tensor_scalar(ex[:, :], ex[:, :], float(E - 1), None, ALU.min))
            dve.tensor_copy(ex_i[:, :], ex[:, :])
            dve.tensor_tensor(first[:, 1:NT], ex[:, 1:NT], ex[:, 0:NT - 1], ALU.not_equal)
            link(dve.memset(first[:, 0:1], 1.0))
            link(dve.tensor_copy(load_i[:, :], first[:, :]))
            assert count[0] == PLAN, count[0]

            with dve.Fori(0, NT) as t:
                dve.wait_ge(x_in, 16 * t + 16)
                dve.wait_ge(added, 16 * t)
                dve.tensor_copy(trow[:, :], xr[:, TOKCOL:TOKCOL + 1])
                dve.tensor_copy(wrow[:, :], xr[:, WCOL:WCOL + 1]).then_inc(meta, 1)
                for q in range(NQ):
                    lo, n = WCH[q]
                    dve.wait_ge(silu, NQ * t + q + 1)
                    dve.tensor_tensor(hh[:, lo:lo + n], gate[q % 2][:, 0:n], pB[q % 2][:, 0:n], ALU.mult)\
                       .then_inc(h_ready, 1)
                dve.wait_ge(down_mm, NQ * t + NQ)
                dve.wait_ge(meta, t + 1)
                dve.tensor_scalar(ow[:, :], pO[:, :], wrow[:, 0:1], None, ALU.mult).then_inc(ow_ready, 1)


def build(nc, x, w_in, conv_w, w_x, w_dt, dt_bias, a_log, d_par, w_out, gate, w1, w2, w3, out):
    rows_d = nc.dram_tensor("rows_d", (DUMMY + P, RW), F32, kind="Internal").ap()
    bc_d = nc.dram_tensor("bc_d", (2 * N, L), F32, kind="Internal").ap()
    cnt_d = nc.dram_tensor("cnt_d", (1, E), F32, kind="Internal").ap()
    mixer(nc, x, w_in, conv_w, w_x, w_dt, dt_bias, a_log, d_par, w_out, gate, out, rows_d, bc_d, cnt_d)
    experts(nc, w1, w2, w3, out, rows_d, cnt_d)


def kernel(**inputs):
    import concourse.bacc as bacc
    from concourse.bass_utils import run_bass_kernel_spmd

    def chunks(a):
        return a.reshape(-1, P, *a.shape[1:]).swapaxes(0, 1)

    g = {k.removeprefix("L0_attn_").removeprefix("L0_ffn_"): np.asarray(v) for k, v in inputs.items()}
    arrays = {
        "x": g["hidden_states"].reshape(TOKENS, D),
        "w_in": chunks(g["in_proj_w"].T),
        "conv_w": chunks(g["conv1d_w"]),
        "w_x": chunks(g["x_proj_w"].T),
        "w_dt": g["dt_proj_w"].T,
        "dt_bias": chunks(g["dt_proj_bias"]),
        "a_log": chunks(g["A_log"]),
        "d_par": chunks(g["D_param"]),
        "w_out": chunks(g["out_proj_w"].T),
        "gate": chunks(g["gate_w"]),
        "w1": g["w1"].reshape(E * D, M),
        "w2": g["w2"].reshape(E * M, D),
        "w3": g["w3"].reshape(E * D, M),
    }
    nc = bacc.Bacc("TRN2", target_bir_lowering=False, num_devices=1)
    feeds, args = {}, []
    for name, a in arrays.items():
        a = np.ascontiguousarray(a)
        feeds[f"in_{name}"] = a
        args.append(nc.dram_tensor(f"in_{name}", a.shape, mybir.dt.from_np(a.dtype), kind="ExternalInput").ap())
    out = nc.dram_tensor("out_0", (TOKENS + P, D), F32, kind="ExternalOutput").ap()
    build(nc, *args, out)
    r = run_bass_kernel_spmd(nc, [feeds], core_ids=[0])
    return r.results[0]["out_0"][:TOKENS].reshape(B, L, D)
```

```python
from contextlib import ExitStack

import numpy as np

import concourse.bass as bass
from concourse import mybir

F32 = mybir.dt.float32
I32 = mybir.dt.int32
ALU = mybir.AluOpType
ACT = mybir.ActivationFunctionType
AXX = mybir.AxisListType.X

P = 128
B, L, D = 8, 512, 512
DIN, N, R, K = 1024, 16, 128, 4
E, M = 8, 1792
EPS = 1e-5

T = 256
STEPS = B * L // T
SPR = L // T
TT = T // P
DC = D // P
CH = DIN // P
UN = 8
UPC = N // UN
SLOTS = CH * UPC
TW = T + 1
PAIRS = CH // 2
QL = 4 * T

TOKENS = B * L
REGION = TOKENS + P
RW = D + 2
TOKCOL, WCOL = D, D + 1
DUMMY = E * REGION
NT = 2 * TOKENS // P + E - 1
PADTOK = TOKENS

WCH = [(0, 512), (512, 512), (1024, 512), (1536, 256)]
NQ = len(WCH)
MK = M // P
LN1P_SMALL = 1.0 / 128


def ge(eng, sem, value):
    if not isinstance(value, int) or value > 0:
        eng.wait_ge(sem, value)


def mixer(nc, x, w_in, conv_w, w_x, w_dt, dt_bias, a_log, d_par, w_out, gate, out, rows_d, bc_d, cnt_d):
    with ExitStack() as ctx:
        sb = lambda name, shape, dt=F32: ctx.enter_context(nc.sbuf_tensor(name, shape, dt))
        pb = lambda name, shape: ctx.enter_context(nc.psum_tensor(name, shape, F32))
        sem = lambda name: ctx.enter_context(nc.semaphore(name))

        wx = sb("wx", [P, CH, R + 2 * N])
        wdt = sb("wdt", [P, DIN])
        wout = sb("wout", [P, CH, D])
        wgate = sb("wgate", [P, DC, E])
        win = [sb(f"win{s}", [P, DC, 4 * P]) for s in range(2)]
        convw = sb("convw", [P, CH, K])
        dtb = sb("dtb", [P, CH])
        dpar = sb("dpar", [P, CH])
        aneg = sb("aneg", [P, CH, N])
        ident = sb("ident", [P, P])
        before = sb("before", [P, P])
        ones = sb("ones", [P, P])
        iota_e = sb("iota_e", [P, TT, E])
        iota_e8 = sb("iota_e8", [P, TT, E])
        ebase = sb("ebase", [P, E])
        tok = sb("tok", [P, TT])

        xf = sb("xf", [P, TT, D])
        xb = sb("xb", [P, TT, D])
        rows = [sb(f"rows{k}", [P, TT, RW]) for k in range(2)]
        xnT = sb("xnT", [P, DC, T])
        xc = [sb(f"xc{s}", [P, CH, T]) for s in range(2)]
        sz = [sb(f"sz{s}", [P, CH, T]) for s in range(2)]
        tail = sb("tail", [P, CH, K - 1])
        state = sb("state", [P, CH, N])
        vsp = sb("vsp", [P, CH * T])
        usp = sb("usp", [P, CH * T])
        delta = sb("delta", [P, CH, T])
        bc = sb("bc", [P, 2 * N, T])
        dA = [sb(f"dA{s}", [P, UN, TW]) for s in range(2)]
        hs = [sb(f"hs{s}", [P, UN, TW]) for s in range(2)]
        tsp = sb("tsp", [P, QL])
        x2T = tsp[:, :].rearrange("p (d t) -> p d t", d=DC)
        dtr = sb("dtr", [P, T])
        bcs = sb("bcs", [2 * N, T])
        dx = sb("dx", [P, T])
        ytmp = sb("ytmp", [P, T])
        st1 = sb("st1", [P, TT, 6])
        mv1 = sb("mv1", [P, TT, 2])
        tiny1 = [sb(f"tiny1{i}", [P, TT]) for i in range(4)]
        st2 = sb("st2", [P, TT, 6])
        mv2 = sb("mv2", [P, TT, 2])
        tiny2 = [sb(f"tiny2{i}", [P, TT]) for i in range(4)]
        lg = sb("lg", [P, TT, E])
        lg2 = sb("lg2", [P, TT, E])
        le = sb("le", [P, TT, E])
        oh = [sb(f"oh{k}", [P, TT, E]) for k in range(2)]
        sel = sb("sel", [P, TT, E])
        pos = sb("pos", [P, TT, E])
        r1 = sb("r1", [P, TT])
        r2 = sb("r2", [P, TT])
        pk = [sb(f"pk{k}", [P, TT]) for k in range(2)]
        posk = [sb(f"posk{k}", [P, TT]) for k in range(2)]
        idx = [sb(f"idx{k}", [P, TT], I32) for k in range(2)]

        pT = [pb(f"pT{s}", [P, DC, P]) for s in range(TT)]
        pM = [pb(f"pM{s}", [P, 2, T]) for s in range(2)]
        pY = [pb(f"pY{s}", [P, 512]) for s in range(2)]
        pO = pb("pO", [P, D])
        pR = pb("pR", [P, 2, TT + 1, E])

        consts_in = sem("consts_in")
        consts_set = sem("consts_set")
        a_exp = sem("a_exp")
        a_neg = sem("a_neg")
        xf_in = sem("xf_in")
        ln1_step = sem("ln1_step")
        var1 = sem("var1")
        sd1 = sem("sd1")
        xn1 = sem("xn1")
        win_in = [sem(f"win_in{s}") for s in range(2)]
        turned1 = sem("turned1")
        tcopied1 = sem("tcopied1")
        x_mm = sem("x_mm")
        tap3 = sem("tap3")
        conv_step = sem("conv_step")
        convolved = sem("convolved")
        xc_ready = sem("xc_ready")
        bc_mm = sem("bc_mm")
        bc_copied = sem("bc_copied")
        bc_stored = sem("bc_stored")
        bc_in = [sem(f"bc_in{i}") for i in range(2 * UPC)]
        dtr_mm = sem("dtr_mm")
        dtr_copied = sem("dtr_copied")
        dt_mm = sem("dt_mm")
        dt_read = sem("dt_read")
        u_ready = sem("u_ready")
        ln_ready = sem("ln_ready")
        sp_step = sem("sp_step")
        delta_ready = sem("delta_ready")
        z_mm = sem("z_mm")
        z_copied = sem("z_copied")
        z_ready = sem("z_ready")
        dx_ready = sem("dx_ready")
        decay = sem("decay")
        inflow = sem("inflow")
        carried = sem("carried")
        scanned = sem("scanned")
        saved = sem("saved")
        weighed = sem("weighed")
        summed = sem("summed")
        ysum_read = [sem(f"ysum_read{j}") for j in range(2)]
        gated = sem("gated")
        xb_in = sem("xb_in")
        out_mm = sem("out_mm")
        x1_ready = sem("x1_ready")
        x1_stored = sem("x1_stored")
        back_step = sem("back_step")
        var2 = sem("var2")
        sd2 = sem("sd2")
        xn2 = sem("xn2")
        turned2 = sem("turned2")
        tcopied2 = sem("tcopied2")
        logits_mm = sem("logits_mm")
        exp_in = sem("exp_in")
        exp_out = sem("exp_out")
        sel_ready = sem("sel_ready")
        rank_mm = sem("rank_mm")
        rows_ready = sem("rows_ready")
        scattered = sem("scattered")
        cnt_stored = sem("cnt_stored")
        pool_turn = sem("pool_turn")
        dve_turn = sem("dve_turn")
        sp_turn = sem("sp_turn")

        NCONST = 9
        NSET = 11
        LN1S, BACKS, SPS = 6, 33, 12
        CONVS = (8 * PAIRS, 12 * PAIRS)

        def each_step(eng, emit):
            for s in (-1, 0):
                emit(s, s % 2)
            with eng.Fori(0, (STEPS - 4) // 2) as i:
                emit(2 * i + 1, 1)
                emit(2 * i + 2, 0)
            for s in range(STEPS - 3, STEPS + 1):
                emit(s, s % 2)

        def has(s):
            if not isinstance(s, int):
                return True, True, True, True
            return 0 <= s < STEPS, s + 1 < STEPS, s + 2 < STEPS, s >= 1

        block = ctx.enter_context(nc.Block())

        @block.sync
        def _(sp):
            def hold(sem_, value):
                if not isinstance(value, int) or value > 0:
                    sp.wait_ge(sem_, value)
                    if not isinstance(value, int):
                        sp.sem_inc(sp_turn, 1)

            def tokens(ap, s):
                return ap[bass.ds(s * T, T), :].rearrange("(t p) d -> p t d", p=P)

            def step(s, odd):
                scan, front, ln1, back = has(s)
                f, r = s + 1, s - 1

                def load_win(j):
                    sp.dma_start(win[j % 2][:, :, :], w_in[:, :, j * 4 * P:(j + 1) * 4 * P]).then_inc(win_in[j % 2], 16)

                if front:
                    hold(z_mm, PAIRS * s + 2)
                    load_win(0)
                if back:
                    hold(x1_stored, 16 * r)
                    hold(xn2, TT * r)
                    sp.dma_start(xb[:, :, :], tokens(x, r)).then_inc(xb_in, 16)
                if front:
                    hold(z_mm, PAIRS * s + 4)
                    load_win(1)
                if ln1:
                    hold(turned1, TT * f + TT)
                    sp.dma_start(xf[:, :, :], tokens(x, s + 2)).then_inc(xf_in, 16)
                if front:
                    hold(x_mm, PAIRS * f + 2)
                    load_win(2)
                    hold(x_mm, PAIRS * f + 4)
                    load_win(3)
                if back:
                    hold(x1_ready, TT * r + TT)
                    sp.dma_start(tokens(out, r), xb[:, :, :]).then_inc(x1_stored, 16)
                if front:
                    hold(bc_copied, f + 1)
                    for i in range(2 * UPC):
                        hold(bc_in[i], 16 * f)
                    sp.dma_start(bc_d, bcs[:, :]).then_inc(bc_stored, 16)
                    hold(bc_stored, 16 * f + 16)
                    for g in range(UPC):
                        for i, used in ((2 * g, inflow), (2 * g + 1, weighed)):
                            hold(used, SLOTS * s + SLOTS - UPC + g + 1)
                            lo = (i % 2) * N + g * UN
                            sp.dma_start(bc[:, lo:lo + UN, :],
                                         bc_d[lo:lo + UN, :].rearrange("(a n) t -> a n t", a=1).to_broadcast([P, UN, T]))\
                              .then_inc(bc_in[i], 16)

            for dst, src in ((wx, w_x), (wdt, w_dt), (wout, w_out), (wgate, gate), (convw, conv_w),
                             (dtb, dt_bias), (dpar, d_par), (aneg, a_log)):
                sp.dma_start(dst[tuple([slice(None)] * len(dst.shape))], src).then_inc(consts_in, 16)
            sp.dma_start(xf[:, :, :], tokens(x, 0)).then_inc(xf_in, 16)
            sp.wait_ge(consts_set, NSET)
            sp.dma_start(out[TOKENS:TOKENS + P, :], tsp[:, 0:D]).then_inc(consts_in, 16)
            each_step(sp, step)
            sp.wait_ge(back_step, BACKS * STEPS)
            sp.dma_start(cnt_d, ebase[0:1, :]).then_inc(cnt_stored, 16)
            sp.wait_ge(cnt_stored, 16)
            sp.wait_ge(x1_stored, 16 * STEPS)
            sp.wait_ge(consts_in, 16 * NCONST)

        @block.gpsimd
        def _(pool):
            pool.memset(tsp[:, :], 0.0).then_inc(consts_set, 1)
            pool.memset(ident[:, :], 0.0).then_inc(consts_set, 1)
            pool.memset(ones[:, :], 1.0).then_inc(consts_set, 1)
            for s in range(2):
                pool.memset(dA[s][:, :, 0:1], 0.0).then_inc(consts_set, 1)
            pool.wait_ge(consts_set, 5)
            pool.affine_select(out=ident[:, :], in_=ident[:, :], compare_op=ALU.not_equal, fill=1.0, base=0,
                               pattern=[[-1, P]], channel_multiplier=1).then_inc(consts_set, 1)
            pool.affine_select(out=before[:, :], in_=ones[:, :], compare_op=ALU.is_gt, fill=0.0, base=0,
                               pattern=[[1, P]], channel_multiplier=-1).then_inc(consts_set, 1)
            pool.iota(iota_e[:, :, :], pattern=[[0, TT], [1, E]], base=0, channel_multiplier=0,
                      allow_small_or_imprecise_dtypes=True).then_inc(consts_set, 1)
            pool.iota(iota_e8[:, :, :], pattern=[[0, TT], [1, E]], base=E, channel_multiplier=0,
                      allow_small_or_imprecise_dtypes=True).then_inc(consts_set, 1)
            pool.iota(ebase[:, :], pattern=[[REGION, E]], base=0, channel_multiplier=0,
                      allow_small_or_imprecise_dtypes=True).then_inc(consts_set, 1)
            pool.iota(tok[:, :], pattern=[[P, TT]], base=0, channel_multiplier=1,
                      allow_small_or_imprecise_dtypes=True).then_inc(consts_set, 1)
            with pool.Fori(0, STEPS) as r:
                pool.wait_ge(rows_ready, r + 1)
                pool.sem_inc(pool_turn, 1)
                for k in range(2):
                    for t in range(TT):
                        pool.indirect_dma_start(
                            out=rows_d, out_offset=bass.IndirectOffsetOnAxis(ap=idx[k][:, t:t + 1], axis=0),
                            in_=rows[k][:, t, :], in_offset=None).then_inc(scattered, 16)
            pool.wait_ge(scattered, 16 * 2 * TT * STEPS)

        @block.scalar
        def _(act):
            def step(s, odd):
                scan, front, ln1, back = has(s)
                f, r = s + 1, s - 1
                xcf, szs, szf = xc[1 - odd], sz[odd], sz[1 - odd]

                def decays(u):
                    c, g = u // UPC, u % UPC
                    if u == 0:
                        ge(act, delta_ready, 2 * s + 1)
                    if u == SLOTS // 2:
                        ge(act, delta_ready, 2 * s + 2)
                    ge(act, scanned, SLOTS * s + u - 1)
                    for i in range(UN):
                        e = act.activation(dA[u % 2][:, i, 1:TW], delta[:, c, :], ACT.Exp,
                                           scale=aneg[:, c, g * UN + i:g * UN + i + 1])
                    e.then_inc(decay, 1)

                def copy_z(pair, n, szn):
                    ge(act, z_mm, PAIRS * n + pair + 1)
                    act.activation(szn[:, 2 * pair:2 * pair + 2, :], pM[pair % 2][:, :, :], ACT.Copy).then_inc(z_copied, 1)

                def beside(u):
                    if u == 0 and scan:
                        copy_z(PAIRS - 1, s, szs)
                    if u == 0 and front:
                        for t in range(TT):
                            ge(act, turned1, TT * f + t + 1)
                            act.activation(xnT[:, :, t * P:(t + 1) * P], pT[t][:, :, :], ACT.Copy).then_inc(tcopied1, 1)
                    if u == 1 and scan:
                        ge(act, z_copied, PAIRS * s + PAIRS)
                        act.activation(szs[:, :, :], szs[:, :, :], ACT.Silu).then_inc(z_ready, 1)
                    if 1 <= u <= PAIRS and front:
                        ge(act, gated, CH * s)
                        ge(act, x_mm, PAIRS * f + u)
                        for h in range(2):
                            c = 2 * (u - 1) + h
                            act.activation(xcf[:, c, :], pM[(u - 1) % 2][:, h, :], ACT.Copy, scale=convw[:, c, K - 1:K])\
                               .then_inc(tap3, 1)
                    if u == PAIRS + 1 and front:
                        ge(act, convolved, PAIRS * f + PAIRS)
                        act.activation(xcf[:, :, :], xcf[:, :, :], ACT.Silu).then_inc(xc_ready, 1)
                    if u == 9 and front:
                        ge(act, bc_mm, f + 1)
                        ge(act, bc_stored, 16 * f)
                        act.activation(bcs[:, :], pM[0][0:2 * N, 0, :], ACT.Copy).then_inc(bc_copied, 1)
                    if u == 9 and back:
                        ge(act, var2, r + 1)
                        act.activation(tiny2[1][:, :], tiny2[0][:, :], ACT.Sqrt).then_inc(sd2, 1)
                    if u == 10 and front:
                        ge(act, dtr_mm, f + 1)
                        act.activation(dtr[:, :], pM[1][:, 0, :], ACT.Copy).then_inc(dtr_copied, 1)
                    if u in (11, 12) and front:
                        half = u - 11
                        ge(act, delta_ready, 2 * f)
                        ge(act, dt_mm, 2 * f + half + 1)
                        for q in range(4):
                            c = 4 * half + q
                            ps, col = pM[q // 2][:, q % 2, :], slice(c * T, (c + 1) * T)
                            act.activation(usp[:, col], ps, ACT.Abs, bias=dtb[:, c:c + 1])
                            i = act.activation(vsp[:, col], ps, ACT.Identity, bias=dtb[:, c:c + 1])
                        i.then_inc(dt_read, 1)
                    if u == 11 and back:
                        for t in range(TT):
                            ge(act, turned2, TT * r + t + 1)
                            ge(act, delta_ready, 2 * s + 2 if scan else 2 * STEPS)
                            act.activation(x2T[:, :, t * P:(t + 1) * P], pT[t][:, :, :], ACT.Copy).then_inc(tcopied2, 1)
                    if u == 12 and front:
                        ge(act, dt_read, 2 * f + 2)
                        act.activation(usp[:, :], usp[:, :], ACT.Exp, scale=-1.0).then_inc(u_ready, 1)
                    if u == 13 and back:
                        ge(act, exp_in, r + 1)
                        act.activation(le[:, :, :], le[:, :, :], ACT.Exp).then_inc(exp_out, 1)
                    if 13 <= u <= 15 and front:
                        copy_z(u - 13, f, szf)
                    if u == 14 and ln1:
                        ge(act, var1, s + 3)
                        act.activation(tiny1[1][:, :], tiny1[0][:, :], ACT.Sqrt).then_inc(sd1, 1)

                if scan:
                    decays(0)
                for u in range(SLOTS):
                    if scan and u + 1 < SLOTS:
                        decays(u + 1)
                    beside(u)
                if front:
                    ge(act, u_ready, f + 1)
                    ge(act, decay, SLOTS * f)
                    ge(act, dx_ready, CH * f)
                    act.activation(delta[:, :, :].rearrange("p c t -> p (c t)"), usp[:, :], ACT.Ln, bias=ones[:, 0:1])\
                       .then_inc(ln_ready, 1)

            act.wait_ge(consts_in, 16 * NCONST)
            act.activation(aneg[:, :, :], aneg[:, :, :], ACT.Exp).then_inc(a_exp, 1)
            act.wait_ge(a_neg, 1)
            act.wait_ge(var1, 1)
            act.activation(tiny1[1][:, :], tiny1[0][:, :], ACT.Sqrt).then_inc(sd1, 1)
            each_step(act, step)

        @block.tensor
        def _(pe):
            def step(s, odd):
                scan, front, ln1, back = has(s)
                f, r = s + 1, s - 1
                xcf, szr = xc[1 - odd], sz[1 - odd]

                def project(ps, wcol, j, h):
                    for d in range(DC):
                        m = pe.matmul(ps[:, h, :], win[j % 2][:, d, wcol:wcol + P], xnT[:, d, :],
                                      start=d == 0, stop=d == DC - 1)
                    return m

                def z_pair(pair, n):
                    if pair >= 2:
                        ge(pe, z_copied, PAIRS * n + pair - 1)
                    else:
                        ge(pe, dt_read, 2 * n + 2)
                    ge(pe, win_in[pair // 2], 16 * (2 * n + 2))
                    for h in range(2):
                        m = project(pM[pair % 2], (pair % 2 * 2 + h) * P, 2 + pair // 2, h)
                    m.then_inc(z_mm, 1)

                def beside(u):
                    if u == 0 and scan:
                        z_pair(PAIRS - 1, s)
                    if u == 0 and front:
                        ge(pe, xn1, TT * f + TT)
                        ge(pe, tcopied2, TT * r)
                        for t in range(TT):
                            for d in range(DC):
                                m = pe.transpose(pT[t][:, d, :], xf[:, t, d * P:(d + 1) * P], ident[:, :])
                            m.then_inc(turned1, 1)
                    if 1 <= u <= PAIRS and front:
                        ge(pe, tcopied1, TT * f + TT)
                        if u <= 2:
                            ge(pe, z_copied, PAIRS * s + 2 + u)
                        else:
                            ge(pe, convolved, PAIRS * f + u - 2)
                        j = (u - 1) // 2
                        ge(pe, win_in[j], 16 * (2 * f + 1))
                        for h in range(2):
                            m = project(pM[(u - 1) % 2], ((u - 1) % 2 * 2 + h) * P, j, h)
                        m.then_inc(x_mm, 1)
                    if 5 <= u <= 8 and back:
                        t, half = (u - 5) // 2, (u - 5) % 2
                        ge(pe, gated, CH * s)
                        ge(pe, x1_ready, TT * r + t)
                        for c in range(4 * half, 4 * half + 4):
                            m = pe.matmul(pO[:, :], szr[:, c, t * P:(t + 1) * P], wout[:, c, :],
                                          start=c == 0, stop=c == CH - 1)
                        if half:
                            m.then_inc(out_mm, 1)
                    if u == 9 and front:
                        ge(pe, xc_ready, f + 1)
                        for c in range(CH):
                            m = pe.matmul(pM[0][0:2 * N, 0, :], wx[:, c, R:R + 2 * N], xcf[:, c, :],
                                          start=c == 0, stop=c == CH - 1)
                        m.then_inc(bc_mm, 1)
                    if u == 10 and front:
                        for c in range(CH):
                            m = pe.matmul(pM[1][:, 0, :], wx[:, c, 0:R], xcf[:, c, :], start=c == 0, stop=c == CH - 1)
                        m.then_inc(dtr_mm, 1)
                    if u in (11, 12) and front:
                        half = u - 11
                        if half == 0:
                            ge(pe, bc_copied, f + 1)
                            ge(pe, dtr_copied, f + 1)
                        else:
                            ge(pe, dt_read, 2 * f + 1)
                        for q in range(4):
                            c = 4 * half + q
                            m = pe.matmul(pM[q // 2][:, q % 2, :], wdt[:, c * P:(c + 1) * P], dtr[:, :], start=True, stop=True)
                        m.then_inc(dt_mm, 1)
                    if u == 11 and back:
                        for t in range(TT):
                            ge(pe, xn2, TT * r + t + 1)
                            for d in range(DC):
                                m = pe.transpose(pT[t][:, d, :], rows[0][:, t, d * P:(d + 1) * P], ident[:, :])
                            m.then_inc(turned2, 1)
                    if u == 12 and back:
                        ge(pe, tcopied2, TT * r + TT)
                        ge(pe, rows_ready, r)
                        for t in range(TT):
                            for d in range(DC):
                                m = pe.matmul(pR[:, 0, t, :], x2T[:, d, t * P:(t + 1) * P], wgate[:, d, :],
                                              start=d == 0, stop=d == DC - 1)
                        m.then_inc(logits_mm, 1)
                    if 13 <= u <= 15 and front:
                        z_pair(u - 13, f)
                    if u == 13 and back:
                        ge(pe, sel_ready, r + 1)
                        for t in range(TT + 1):
                            for q in range(min(t + 1, TT)):
                                m = pe.matmul(pR[:, 1, t, :], before[:, :] if q == t else ones[:, :], sel[:, q, :],
                                              start=q == 0, stop=q == min(t, TT - 1))
                        m.then_inc(rank_mm, 1)

                for u in range(SLOTS):
                    beside(u)
                    if scan:
                        c, g = u // UPC, u % UPC
                        if g == 0:
                            ge(pe, ysum_read[c % 2], CH // 2 * s + c // 2)
                        ge(pe, weighed, SLOTS * s + u + 1)
                        for i in range(UN):
                            m = pe.matmul(pY[c % 2][:, 0:T], ident[:, :], hs[u % 2][:, i, 1:TW],
                                          start=g == 0 and i == 0, stop=g == UPC - 1 and i == UN - 1)
                        m.then_inc(summed, 1)

            pe.wait_ge(consts_in, 16 * NCONST)
            pe.wait_ge(consts_set, NSET)
            each_step(pe, step)

        @block.vector
        def _(dve):
            class Chain:
                def __init__(self, sem_, base):
                    self.sem, self.base, self.n = sem_, base, 0

                def link(self, ins):
                    self.n += 1
                    ins.then_inc(self.sem, 1)
                    dve.wait_ge(self.sem, self.base + self.n)

            def norm_stats(ch, src, st, mv, tiny, ready):
                for t in range(TT):
                    i = dve.bn_stats(st[:, t, :], src[:, t, :])
                ch.link(i)
                dve.sem_inc(dve_turn, 1)
                for t in range(TT):
                    i = dve.bn_aggr(mv[:, t, :], st[:, t, :])
                ch.link(i)
                dve.tensor_scalar(tiny[0][:, :], mv[:, :, 1], EPS, None, ALU.add).then_inc(ready, 1)

            def norm_scale(ch, tiny):
                ve, sd, rs, nt = tiny
                ch.link(dve.reciprocal(rs[:, :], sd[:, :]))
                ch.link(dve.tensor_tensor(nt[:, :], rs[:, :], rs[:, :], ALU.mult))
                ch.link(dve.scalar_tensor_tensor(nt[:, :], nt[:, :], -0.5, ve[:, :], ALU.mult, ALU.mult))
                ch.link(dve.scalar_tensor_tensor(rs[:, :], nt[:, :], 1.5, rs[:, :], ALU.add, ALU.mult))

            def normalise(dst, src, mv, tiny, t):
                return dve.tensor_scalar(dst, src, mv[:, t, 0:1], tiny[2][:, t:t + 1], ALU.subtract, ALU.mult)

            def ln1_first(n):
                dve.wait_ge(xf_in, 16 * n + 16)
                ch = Chain(ln1_step, LN1S * n)
                norm_stats(ch, xf, st1, mv1, tiny1, var1)

            def ln1_second(n):
                ch = Chain(ln1_step, LN1S * n + 2)
                dve.wait_ge(sd1, n + 1)
                norm_scale(ch, tiny1)
                for t in range(TT):
                    normalise(xf[:, t, :], xf[:, t, :], mv1, tiny1, t).then_inc(xn1, 1)
                assert ch.n == LN1S - 2

            def convolve(pair, f, fodd, xcf):
                base = (CONVS[0] + CONVS[1]) // 2 * (f - fodd) + CONVS[0] * fodd + CONVS[fodd] // PAIRS * pair
                ge(dve, tap3, CH * f + 2 * pair + 2)
                n = 0

                def done(ins):
                    nonlocal n
                    n += 1
                    return ins.then_inc(conv_step, 1)

                for k in range(K - 1):
                    s = K - 1 - k
                    for h in range(2):
                        c = 2 * pair + h
                        if k:
                            dve.wait_ge(conv_step, base + n - 1)
                        done(dve.scalar_tensor_tensor(xcf[:, c, s:T], pM[pair % 2][:, h, 0:T - s], convw[:, c, k:k + 1],
                                                      xcf[:, c, s:T], ALU.mult, ALU.add))
                if fodd:
                    for k in range(K - 1):
                        s = K - 1 - k
                        for h in range(2):
                            c = 2 * pair + h
                            dve.wait_ge(conv_step, base + n - 1)
                            i = done(dve.scalar_tensor_tensor(xcf[:, c, 0:s], tail[:, c, K - 1 - s:K - 1], convw[:, c, k:k + 1],
                                                              xcf[:, c, 0:s], ALU.mult, ALU.add))
                else:
                    for h in range(2):
                        i = done(dve.tensor_copy(tail[:, 2 * pair + h, :], pM[pair % 2][:, h, T - K + 1:T]))
                dve.wait_ge(conv_step, base + n)
                dve.sem_inc(convolved, 1)
                assert n == CONVS[fodd] // PAIRS

            def softplus(f):
                ch = Chain(sp_step, SPS * f)
                ge(dve, u_ready, f + 1)
                ge(dve, ln_ready, f + 1)
                dflat = delta[:, :, :].rearrange("p c t -> p (c t)")
                for j in range(2):
                    part = slice(j * QL, (j + 1) * QL)
                    ch.link(dve.tensor_scalar(tsp[:, :], usp[:, part], 1.0 / 3, -0.5, ALU.mult, ALU.add))
                    ch.link(dve.tensor_tensor(tsp[:, :], tsp[:, :], usp[:, part], ALU.mult))
                    ch.link(dve.scalar_tensor_tensor(tsp[:, :], tsp[:, :], 1.0, usp[:, part], ALU.add, ALU.mult))
                    ch.link(dve.tensor_scalar(usp[:, part].bitcast(I32), usp[:, part], LN1P_SMALL, None, ALU.is_lt))
                    dve.sem_inc(dve_turn, 1)
                    ch.link(dve.copy_predicated(dflat[:, part], usp[:, part].bitcast(I32), tsp[:, :]))
                    ch.link(dve.scalar_tensor_tensor(dflat[:, part], vsp[:, part], 0.0, dflat[:, part], ALU.max, ALU.add))
                    dve.sem_inc(delta_ready, 1)
                assert ch.n == SPS

            def step(s, odd):
                scan, front, ln1, back = has(s)
                f, r = s + 1, s - 1
                xcs = xc[odd]

                def unit(u):
                    c, g = u // UPC, u % UPC
                    k = SLOTS * s + u
                    if g == 0:
                        ge(dve, inflow, k)
                        dve.tensor_tensor(dx[:, :], delta[:, c, :], xcs[:, c, :], ALU.mult).then_inc(dx_ready, 1)
                    if c == 0:
                        ge(dve, bc_in[2 * g], 16 * s + 16)
                    ge(dve, summed, k - 1)
                    row0 = hs[u % 2][:, :, 0:1]
                    if odd:
                        i = dve.tensor_copy(row0, state[:, c, g * UN:(g + 1) * UN].rearrange("p (n a) -> p n a", a=1))
                    else:
                        i = dve.memset(row0, 0.0)
                    i.then_inc(carried, 1)
                    ge(dve, dx_ready, CH * s + c + 1)
                    dve.tensor_tensor(hs[u % 2][:, :, 1:TW], dx[:, :].rearrange("p (a t) -> p a t", a=1).to_broadcast([P, UN, T]),
                                      bc[:, g * UN:(g + 1) * UN, :], ALU.mult).then_inc(inflow, 1)
                    ge(dve, decay, k + 1)
                    ge(dve, carried, k + 1)
                    ge(dve, inflow, k + 1)
                    flat = hs[u % 2][:, :, :].rearrange("p n t -> p (n t)")
                    dve.tensor_tensor_scan(flat, dA[u % 2][:, :, :].rearrange("p n t -> p (n t)"), flat, 0.0,
                                           ALU.mult, ALU.add).then_inc(scanned, 1)
                    if g == 0 and c >= 1:
                        finish(s, c - 1, odd)
                    ge(dve, scanned, k + 1)
                    if not odd:
                        dve.tensor_copy(state[:, c, g * UN:(g + 1) * UN].rearrange("p (n a) -> p n a", a=1),
                                        hs[u % 2][:, :, T:TW]).then_inc(saved, 1)
                        ge(dve, saved, SLOTS // 2 * s + u + 1)
                    if c == 0:
                        ge(dve, bc_in[2 * g + 1], 16 * s + 16)
                    dve.tensor_tensor(hs[u % 2][:, :, 1:TW], hs[u % 2][:, :, 1:TW], bc[:, N + g * UN:N + (g + 1) * UN, :],
                                      ALU.mult).then_inc(weighed, 1)

                def finish(n, c, nodd):
                    ge(dve, summed, SLOTS * n + UPC * (c + 1))
                    ge(dve, z_ready, n + 1)
                    ge(dve, gated, CH * n + c)
                    dve.scalar_tensor_tensor(ytmp[:, :], xc[nodd][:, c, :], dpar[:, c:c + 1], pY[c % 2][:, 0:T],
                                             ALU.mult, ALU.add).then_inc(ysum_read[c % 2], 1)
                    ge(dve, ysum_read[c % 2], CH // 2 * n + c // 2 + 1)
                    dve.tensor_tensor(sz[nodd][:, c, :], ytmp[:, :], sz[nodd][:, c, :], ALU.mult).then_inc(gated, 1)

                spread = lambda v: v[:, :].rearrange("p (t a) -> p t a", a=1).to_broadcast([P, TT, E])

                def residual(t):
                    ge(dve, xb_in, 16 * r + 16)
                    ge(dve, out_mm, TT * r + t + 1)
                    dve.tensor_tensor(xb[:, t, :], pO[:, :], xb[:, t, :], ALU.add).then_inc(x1_ready, 1)

                def route_first(ch):
                    ge(dve, logits_mm, r + 1)
                    ch.link(dve.tensor_copy(lg[:, :, :], pR[:, 0, 0:TT, :]))
                    src = lg
                    for k in range(2):
                        ch.link(dve.tensor_reduce(r1[:, :], src[:, :, :], AXX, ALU.max))
                        if k == 0:
                            dve.tensor_tensor(le[:, :, :], lg[:, :, :], spread(r1), ALU.subtract).then_inc(exp_in, 1)
                        ch.link(dve.tensor_tensor(oh[k][:, :, :], src[:, :, :], spread(r1), ALU.is_equal))
                        ch.link(dve.scalar_tensor_tensor(oh[k][:, :, :], oh[k][:, :, :], -float(E), iota_e8[:, :, :],
                                                         ALU.mult, ALU.add))
                        ch.link(dve.tensor_reduce(r1[:, :], oh[k][:, :, :], AXX, ALU.min))
                        ch.link(dve.tensor_tensor(oh[k][:, :, :], iota_e[:, :, :], spread(r1), ALU.is_equal))
                        if k == 0:
                            ch.link(dve.scalar_tensor_tensor(lg2[:, :, :], oh[0][:, :, :], -3.0e38, lg[:, :, :],
                                                             ALU.mult, ALU.add))
                            src = lg2
                    dve.tensor_tensor(sel[:, :, :], oh[0][:, :, :], oh[1][:, :, :], ALU.add).then_inc(sel_ready, 1)

                def route_second(ch):
                    ge(dve, exp_out, r + 1)
                    ch.link(dve.tensor_reduce(r1[:, :], le[:, :, :], AXX, ALU.add))
                    ch.link(dve.reciprocal(r2[:, :], r1[:, :]))
                    ch.link(dve.tensor_tensor(le[:, :, :], le[:, :, :], spread(r2), ALU.mult))
                    for k in range(2):
                        ch.link(dve.tensor_tensor(lg2[:, :, :], le[:, :, :], oh[k][:, :, :], ALU.mult))
                        ch.link(dve.tensor_reduce(pk[k][:, :], lg2[:, :, :], AXX, ALU.add))
                    ch.link(dve.tensor_tensor(r1[:, :], pk[0][:, :], pk[1][:, :], ALU.add))
                    ch.link(dve.reciprocal(r1[:, :], r1[:, :]))
                    for k in range(2):
                        dve.tensor_tensor(rows[k][:, :, WCOL], pk[k][:, :], r1[:, :], ALU.mult)
                        dve.tensor_copy(rows[k][:, :, TOKCOL], tok[:, :])
                    ge(dve, rank_mm, r + 1)
                    base = ebase[:, :].rearrange("p (a e) -> p a e", a=1).to_broadcast([P, TT, E])
                    ch.link(dve.tensor_tensor(pos[:, :, :], pR[:, 1, 0:TT, :], base, ALU.add))
                    for k in range(2):
                        ch.link(dve.tensor_tensor(lg2[:, :, :], pos[:, :, :], oh[k][:, :, :], ALU.mult))
                        ch.link(dve.tensor_reduce(posk[k][:, :], lg2[:, :, :], AXX, ALU.add))
                        i = dve.tensor_copy(idx[k][:, :], posk[k][:, :])
                    ch.link(dve.tensor_tensor(ebase[:, :], ebase[:, :], pR[:, 1, TT, :], ALU.add))
                    dve.tensor_scalar(tok[:, :], tok[:, :], float(T), None, ALU.add).then_inc(rows_ready, 1)

                back_chain = Chain(back_step, BACKS * r)

                def beside(u):
                    if 1 <= u <= PAIRS and front:
                        convolve(u - 1, f, 1 - odd, xc[1 - odd])
                    if u == 6 and back:
                        residual(0)
                    if u == 8 and back:
                        residual(1)
                        ge(dve, x1_ready, TT * r + TT)
                        norm_stats(back_chain, xb, st2, mv2, tiny2, var2)
                    if u == 10 and back:
                        ge(dve, sd2, r + 1)
                        norm_scale(back_chain, tiny2)
                        ge(dve, scattered, 16 * 2 * TT * r)
                        for t in range(TT):
                            normalise(rows[1][:, t, 0:D], xb[:, t, :], mv2, tiny2, t)
                            normalise(rows[0][:, t, 0:D], xb[:, t, :], mv2, tiny2, t).then_inc(xn2, 1)
                    if u == 12 and back:
                        route_first(back_chain)
                    if u == 14 and back:
                        route_second(back_chain)
                        assert back_chain.n == BACKS, back_chain.n
                    if u == 13 and ln1:
                        ln1_first(s + 2)
                    if u == 15 and ln1:
                        ln1_second(s + 2)

                for u in range(SLOTS):
                    if scan:
                        unit(u)
                    if u == 0 and back:
                        finish(r, CH - 1, 1 - odd)
                    beside(u)
                if front:
                    softplus(f)

            dve.wait_ge(a_exp, 1)
            dve.wait_ge(consts_set, NSET)
            dve.tensor_scalar(aneg[:, :, :], aneg[:, :, :], -1.0, None, ALU.mult).then_inc(a_neg, 1)
            dve.wait_ge(consts_in, 16 * NCONST)
            ln1_first(0)
            ln1_second(0)
            each_step(dve, step)


def experts(nc, w1, w2, w3, out, rows_d, cnt_d):
    with ExitStack() as ctx:
        sb = lambda name, shape, dt=F32: ctx.enter_context(nc.sbuf_tensor(name, shape, dt))
        pb = lambda name, shape: ctx.enter_context(nc.psum_tensor(name, shape, F32))
        sem = lambda name: ctx.enter_context(nc.semaphore(name))

        w1s = sb("w1s", [P, DC, M])
        w3s = sb("w3s", [P, DC, M])
        w2s = sb("w2s", [P, MK, D])
        ident = sb("ident2", [P, P])
        xr = sb("xr", [P, RW])
        xT = sb("xT", [P, DC, P])
        gate = [sb(f"gate{s}", [P, 512]) for s in range(2)]
        hh = sb("hh", [P, M])
        hT = sb("hT", [P, MK, P])
        wrow = sb("wrow", [P, 1])
        trow = sb("trow", [P, 1], I32)
        ow = sb("ow", [P, D])
        pad = sb("pad", [P, RW])
        ptok = sb("ptok", [P, 1])
        ends = sb("ends", [1, E])
        cnt = sb("cnt", [1, E])
        ci = sb("ci", [1, E], I32)
        tiles = sb("tiles", [1, E])
        ebase = sb("ebase2", [1, E])
        tnum = sb("tnum", [1, NT, E])
        over = sb("over", [1, NT, E])
        ex = sb("ex", [1, NT])
        used = sb("used", [1, NT])
        tn = sb("tn", [1, NT])
        first = sb("first", [1, NT])
        one8 = sb("one8", [1, E])
        row_i = sb("row_i", [1, NT], I32)
        ex_i = sb("ex_i", [1, NT], I32)
        load_i = sb("load_i", [1, NT], I32)
        pad_i = sb("pad_i", [1, E + 1], I32)

        pA = [pb(f"pA{s}", [P, 512]) for s in range(2)]
        pB = [pb(f"pB{s}", [P, 512]) for s in range(2)]
        pH = [pb(f"pH{s}", [P, 4, P]) for s in range(2)]
        pX = pb("pX", [P, DC, P])
        pO = pb("pD", [P, D])

        cnt_in = sem("cnt_in")
        set_up = sem("set_up")
        plan = sem("plan")
        padded = sem("padded")
        x_in = sem("x_in2")
        w13_in = [sem(f"w13_in{q}") for q in range(NQ)]
        w2_in = [sem(f"w2_in{q}") for q in range(NQ)]
        x_turned = sem("x_turned")
        x_copied = sem("x_copied")
        meta = sem("meta")
        up_mm = sem("up_mm")
        silu = sem("silu")
        h_ready = sem("h_ready")
        h_turned = sem("h_turned")
        h_copied = sem("h_copied")
        down_mm = sem("down_mm")
        ow_ready = sem("ow_ready")
        added = sem("added")
        turn = sem("turn2")

        PLAN = 18
        block = ctx.enter_context(nc.Block())

        @block.gpsimd
        def _(pool):
            pool.memset(ident[:, :], 0.0).then_inc(set_up, 1)
            pool.memset(pad[:, :], 0.0).then_inc(set_up, 1)
            pool.memset(one8[:, :], 1.0).then_inc(set_up, 1)
            pool.wait_ge(set_up, 3)
            pool.affine_select(out=ident[:, :], in_=ident[:, :], compare_op=ALU.not_equal, fill=1.0, base=0,
                               pattern=[[-1, P]], channel_multiplier=1).then_inc(set_up, 1)
            pool.iota(ptok[:, :], pattern=[[0, 1]], base=PADTOK, channel_multiplier=1,
                      allow_small_or_imprecise_dtypes=True).then_inc(set_up, 1)
            pool.iota(tnum[:, :, :], pattern=[[1, NT], [0, E]], base=0, channel_multiplier=0,
                      allow_small_or_imprecise_dtypes=True).then_inc(set_up, 1)
            pool.iota(tn[:, :], pattern=[[1, NT]], base=0, channel_multiplier=0,
                      allow_small_or_imprecise_dtypes=True).then_inc(set_up, 1)
            pool.iota(ebase[:, :], pattern=[[REGION, E]], base=0, channel_multiplier=0,
                      allow_small_or_imprecise_dtypes=True).then_inc(set_up, 1)
            def add_rows(t):
                ge(pool, ow_ready, t + 1)
                ge(pool, added, 16 * t)
                pool.sem_inc(turn, 1)
                pool.indirect_dma_start(out=out, out_offset=bass.IndirectOffsetOnAxis(ap=trow[:, 0:1], axis=0),
                                        in_=ow[:, :], in_offset=None, compute_op=ALU.add).then_inc(added, 16)

            add_rows(0)
            with pool.Fori(1, NT) as t:
                add_rows(t)
            pool.wait_ge(added, 16 * NT)

        @block.sync
        def _(sp):
            sp.dma_start(cnt[:, :], cnt_d).then_inc(cnt_in, 16)
            sp.wait_ge(plan, PLAN)
            with sp.Fori(0, E + 1) as e:
                r = sp.value_load(pad_i[0:1, bass.ds(e, 1)], min_val=0, max_val=DUMMY)
                sp.dma_start(rows_d[bass.ds(r, P), :], pad[:, :]).then_inc(padded, 16)
            sp.wait_ge(padded, 16 * (E + 1))

            def load_rows(t):
                r = sp.value_load(row_i[0:1, bass.ds(t, 1)], min_val=0, max_val=DUMMY)
                sp.dma_start(xr[:, :], rows_d[bass.ds(r, P), :]).then_inc(x_in, 16)

            def load_up(q, e, c=None):
                lo, n = WCH[q]
                for ws, w in ((w1s, w1), (w3s, w3)):
                    src = w[bass.ds(e * D, D), lo:lo + n].rearrange("(c p) m -> p c m", p=P)
                    if c is None:
                        sp.dma_start(ws[:, :, lo:lo + n], src).then_inc(w13_in[q], 16)
                    else:
                        sp.dma_start(ws[:, :, lo:lo + n], src, cond=c, bounds_check="skip_entire_dma")\
                          .then_inc(w13_in[q], 16)

            def load_down(q, e, c=None):
                lo, n = WCH[q][0] // P, WCH[q][1] // P
                src = w2[bass.ds(e * M + lo * P, n * P), :].rearrange("(k p) d -> p k d", p=P)
                if c is None:
                    sp.dma_start(w2s[:, lo:lo + n, :], src).then_inc(w2_in[q], 16)
                else:
                    sp.dma_start(w2s[:, lo:lo + n, :], src, cond=c, bounds_check="skip_entire_dma")\
                      .then_inc(w2_in[q], 16)

            load_rows(0)
            e0 = sp.value_load(ex_i[0:1, 0:1], min_val=0, max_val=E - 1)
            for q in range(NQ):
                load_up(q, e0)
            for q in range(NQ):
                load_down(q, e0)
            with sp.Fori(0, NT - 1) as t:
                sp.wait_ge(x_turned, t + 1)
                sp.wait_ge(meta, t + 1)
                load_rows(t + 1)
                e1 = sp.value_load(ex_i[0:1, bass.ds(t + 1, 1)], min_val=0, max_val=E - 1)
                new = sp.value_load(load_i[0:1, bass.ds(t + 1, 1)], min_val=0, max_val=1)
                for q in range(NQ):
                    sp.wait_ge(up_mm, NQ * t + q + 1)
                    load_up(q, e1, new > 0)
                for q in range(NQ):
                    sp.wait_ge(down_mm, NQ * t + q + 1)
                    load_down(q, e1, new > 0)

        @block.scalar
        def _(act):
            def tile(t, last):
                def silu_q(q):
                    n = WCH[q][1]
                    act.wait_ge(up_mm, NQ * t + q + 1)
                    ge(act, h_ready, NQ * t + max(q - 1, 0))
                    act.activation(gate[q % 2][:, 0:n], pA[q % 2][:, 0:n], ACT.Silu).then_inc(silu, 1)

                def copy_q(q):
                    lo, n = WCH[q][0] // P, WCH[q][1] // P
                    act.wait_ge(h_turned, NQ * t + q + 1)
                    act.activation(hT[:, lo:lo + n, :], pH[q % 2][:, 0:n, :], ACT.Copy).then_inc(h_copied, 1)

                silu_q(0)
                for q in range(1, NQ):
                    silu_q(q)
                    copy_q(q - 1)
                if not last:
                    act.wait_ge(x_turned, t + 2)
                    act.activation(xT[:, :, :], pX[:, :, :], ACT.Copy).then_inc(x_copied, 1)
                copy_q(NQ - 1)

            act.wait_ge(x_turned, 1)
            act.activation(xT[:, :, :], pX[:, :, :], ACT.Copy).then_inc(x_copied, 1)
            tile(0, False)
            with act.Fori(1, NT - 1) as t:
                tile(t, False)
            tile(NT - 1, True)

        @block.tensor
        def _(pe):
            def turn_rows(t):
                pe.wait_ge(x_in, 16 * t + 16)
                for d in range(DC):
                    m = pe.transpose(pX[:, d, :], xr[:, d * P:(d + 1) * P], ident[:, :])
                m.then_inc(x_turned, 1)

            def tile(t, last):
                def up(q):
                    lo, n = WCH[q]
                    pe.wait_ge(w13_in[q], 32 * t + 32)
                    ge(pe, h_ready, NQ * t + max(q - 1, 0))
                    for ps, ws in ((pA, w1s), (pB, w3s)):
                        for d in range(DC):
                            m = pe.matmul(ps[q % 2][:, 0:n], xT[:, d, :], ws[:, d, lo:lo + n],
                                          start=d == 0, stop=d == DC - 1)
                    m.then_inc(up_mm, 1)

                def turn_h(q):
                    pe.wait_ge(h_ready, NQ * t + q + 1)
                    ge(pe, h_copied, NQ * t + max(q - 1, 0))
                    lo, n = WCH[q][0] // P, WCH[q][1] // P
                    for k in range(n):
                        m = pe.transpose(pH[q % 2][:, k, :], hh[:, (lo + k) * P:(lo + k + 1) * P], ident[:, :])
                    m.then_inc(h_turned, 1)

                def down(q):
                    lo, n = WCH[q][0] // P, WCH[q][1] // P
                    pe.wait_ge(h_copied, NQ * t + q + 1)
                    pe.wait_ge(w2_in[q], 16 * t + 16)
                    for k in range(lo, lo + n):
                        m = pe.matmul(pO[:, :], hT[:, k, :], w2s[:, k, :], start=k == 0, stop=k == MK - 1)
                    m.then_inc(down_mm, 1)

                pe.wait_ge(x_copied, t + 1)
                up(0)
                for q in range(1, NQ):
                    up(q)
                    turn_h(q - 1)
                if not last:
                    turn_rows(t + 1)
                ge(pe, ow_ready, t)
                for q in range(NQ - 1):
                    down(q)
                turn_h(NQ - 1)
                down(NQ - 1)

            pe.wait_ge(set_up, 8)
            turn_rows(0)
            tile(0, False)
            with pe.Fori(1, NT - 1) as t:
                tile(t, False)
            tile(NT - 1, True)

        @block.vector
        def _(dve):
            count = [0]

            def link(ins):
                count[0] += 1
                ins.then_inc(plan, 1)
                dve.wait_ge(plan, count[0])

            dve.wait_ge(set_up, 8)
            dve.wait_ge(cnt_in, 16)
            link(dve.tensor_copy(pad[:, TOKCOL:TOKCOL + 1], ptok[:, :]))
            link(dve.tensor_copy(pad_i[:, 0:E], cnt[:, :]))
            link(dve.memset(pad_i[:, E:E + 1], DUMMY))
            link(dve.tensor_tensor(ends[:, :], cnt[:, :], ebase[:, :], ALU.subtract))
            link(dve.tensor_scalar(ci[:, :], ends[:, :], float(P - 1), None, ALU.add))
            link(dve.tensor_scalar(ci[:, :], ci[:, :], P.bit_length() - 1, None, ALU.logical_shift_right))
            link(dve.tensor_copy(tiles[:, :], ci[:, :]))
            link(dve.tensor_tensor_scan(ends[:, :], one8[:, :], tiles[:, :], 0.0, ALU.mult, ALU.add))
            wide = lambda v: v[:, :].rearrange("p (a e) -> p a e", a=1).to_broadcast([1, NT, E])
            link(dve.tensor_tensor(over[:, :, :], tnum[:, :, :], wide(ends), ALU.is_ge))
            link(dve.tensor_reduce(ex[:, :], over[:, :, :], AXX, ALU.add))
            link(dve.tensor_tensor(over[:, :, :], over[:, :, :], wide(tiles), ALU.mult))
            link(dve.tensor_reduce(used[:, :], over[:, :, :], AXX, ALU.add))
            link(dve.tensor_tensor(used[:, :], tn[:, :], used[:, :], ALU.subtract))
            link(dve.tensor_scalar(used[:, :], used[:, :], float(P), None, ALU.mult))
            link(dve.scalar_tensor_tensor(used[:, :], ex[:, :], float(REGION), used[:, :], ALU.mult, ALU.add))
            dve.tensor_scalar(row_i[:, :], used[:, :], float(DUMMY), None, ALU.min)
            link(dve.tensor_scalar(ex[:, :], ex[:, :], float(E - 1), None, ALU.min))
            dve.tensor_copy(ex_i[:, :], ex[:, :])
            dve.tensor_tensor(first[:, 1:NT], ex[:, 1:NT], ex[:, 0:NT - 1], ALU.not_equal)
            link(dve.memset(first[:, 0:1], 1.0))
            link(dve.tensor_copy(load_i[:, :], first[:, :]))
            assert count[0] == PLAN, count[0]

            def tile(t):
                dve.wait_ge(x_in, 16 * t + 16)
                ge(dve, added, 16 * t)
                dve.tensor_copy(trow[:, :], xr[:, TOKCOL:TOKCOL + 1])
                dve.tensor_copy(wrow[:, :], xr[:, WCOL:WCOL + 1]).then_inc(meta, 1)
                for q in range(NQ):
                    lo, n = WCH[q]
                    dve.wait_ge(silu, NQ * t + q + 1)
                    dve.tensor_tensor(hh[:, lo:lo + n], gate[q % 2][:, 0:n], pB[q % 2][:, 0:n], ALU.mult)\
                       .then_inc(h_ready, 1)
                dve.wait_ge(down_mm, NQ * t + NQ)
                dve.wait_ge(meta, t + 1)
                dve.tensor_scalar(ow[:, :], pO[:, :], wrow[:, 0:1], None, ALU.mult).then_inc(ow_ready, 1)

            tile(0)
            with dve.Fori(1, NT) as t:
                tile(t)


def build(nc, x, w_in, conv_w, w_x, w_dt, dt_bias, a_log, d_par, w_out, gate, w1, w2, w3, out):
    rows_d = nc.dram_tensor("rows_d", (DUMMY + P, RW), F32, kind="Internal").ap()
    bc_d = nc.dram_tensor("bc_d", (2 * N, T), F32, kind="Internal").ap()
    cnt_d = nc.dram_tensor("cnt_d", (1, E), F32, kind="Internal").ap()
    mixer(nc, x, w_in, conv_w, w_x, w_dt, dt_bias, a_log, d_par, w_out, gate, out, rows_d, bc_d, cnt_d)
    experts(nc, w1, w2, w3, out, rows_d, cnt_d)


def kernel(**inputs):
    import concourse.bacc as bacc
    from concourse.bass_utils import run_bass_kernel_spmd

    def chunks(a):
        return a.reshape(-1, P, *a.shape[1:]).swapaxes(0, 1)

    g = {k.removeprefix("L0_attn_").removeprefix("L0_ffn_"): np.asarray(v) for k, v in inputs.items()}
    arrays = {
        "x": g["hidden_states"].reshape(TOKENS, D),
        "w_in": chunks(g["in_proj_w"].T),
        "conv_w": chunks(g["conv1d_w"]),
        "w_x": chunks(g["x_proj_w"].T),
        "w_dt": g["dt_proj_w"].T,
        "dt_bias": chunks(g["dt_proj_bias"]),
        "a_log": chunks(g["A_log"]),
        "d_par": chunks(g["D_param"]),
        "w_out": chunks(g["out_proj_w"].T),
        "gate": chunks(g["gate_w"]),
        "w1": g["w1"].reshape(E * D, M),
        "w2": g["w2"].reshape(E * M, D),
        "w3": g["w3"].reshape(E * D, M),
    }
    nc = bacc.Bacc("TRN2", target_bir_lowering=False, num_devices=1)
    feeds, args = {}, []
    for name, a in arrays.items():
        a = np.ascontiguousarray(a)
        feeds[f"in_{name}"] = a
        args.append(nc.dram_tensor(f"in_{name}", a.shape, mybir.dt.from_np(a.dtype), kind="ExternalInput").ap())
    out = nc.dram_tensor("out_0", (TOKENS + P, D), F32, kind="ExternalOutput").ap()
    build(nc, *args, out)
    r = run_bass_kernel_spmd(nc, [feeds], core_ids=[0])
    return r.results[0]["out_0"][:TOKENS].reshape(B, L, D)
```

```python
from contextlib import ExitStack

import numpy as np

import concourse.bass as bass
from concourse import mybir

F32 = mybir.dt.float32
I32 = mybir.dt.int32
ALU = mybir.AluOpType
ACT = mybir.ActivationFunctionType
AXX = mybir.AxisListType.X

P = 128
B, L, D = 8, 512, 512
DIN, N, R, K = 1024, 16, 128, 4
E, M = 8, 1792
EPS = 1e-5

T = 256
STEPS = B * L // T
SPR = L // T
TT = T // P
DC = D // P
CH = DIN // P
UN = 8
UPC = N // UN
SLOTS = CH * UPC
TW = T + 1
PAIRS = CH // 2

TOKENS = B * L
REGION = TOKENS + P
RW = D + 2
TOKCOL, WCOL = D, D + 1
DUMMY = E * REGION
NT = 2 * TOKENS // P + E - 1
NT_SURE = 2 * TOKENS // P
PADTOK = TOKENS

WCH = [(0, 512), (512, 512), (1024, 512), (1536, 256)]
NQ = len(WCH)
MK = M // P
LN1P_SMALL = 1.0 / 128
LN1P_SLOPE = 1.0 / 3 ** 0.5
LN1P_SHIFT = -0.25 / LN1P_SLOPE
LN1P_REST = 1.0 - LN1P_SHIFT ** 2


def ge(eng, sem, value):
    if not isinstance(value, int) or value > 0:
        eng.wait_ge(sem, value)


def mixer(nc, x, w_in, conv_w, w_x, w_dt, dt_bias, a_log, d_par, w_out, gate, out, rows_d, bc_d, cnt_d):
    with ExitStack() as ctx:
        sb = lambda name, shape, dt=F32: ctx.enter_context(nc.sbuf_tensor(name, shape, dt))
        pb = lambda name, shape: ctx.enter_context(nc.psum_tensor(name, shape, F32))
        sem = lambda name: ctx.enter_context(nc.semaphore(name))

        wx = sb("wx", [P, CH, R + 2 * N])
        wdt = sb("wdt", [P, DIN])
        wout = sb("wout", [P, CH, D])
        wgate = sb("wgate", [P, DC, E])
        win = [sb(f"win{s}", [P, DC, 4 * P]) for s in range(2)]
        convw = sb("convw", [P, CH, K])
        dtb = sb("dtb", [P, CH])
        dpar = sb("dpar", [P, CH])
        aneg = sb("aneg", [P, CH, N])
        ident = sb("ident", [P, P])
        before = sb("before", [P, P])
        ones = sb("ones", [P, P])
        iota_e = sb("iota_e", [P, TT, E])
        iota_e8 = sb("iota_e8", [P, TT, E])
        ebase = sb("ebase", [P, E])
        tok = sb("tok", [P, TT])

        xf = sb("xf", [P, TT, D])
        xb = sb("xb", [P, TT, D])
        rows = [sb(f"rows{k}", [P, TT, RW]) for k in range(2)]
        xnT = [sb(f"xnT{s}", [P, DC, T]) for s in range(2)]
        xc = [sb(f"xc{s}", [P, CH, T]) for s in range(2)]
        sz = [sb(f"sz{s}", [P, CH, T]) for s in range(2)]
        tail = sb("tail", [P, CH, K - 1])
        state = sb("state", [P, CH, N])
        vsp = sb("vsp", [P, CH * T])
        usp = sb("usp", [P, CH * T])
        delta = sb("delta", [P, CH, T])
        bc = sb("bc", [P, 2 * N, T])
        dA = [sb(f"dA{s}", [P, UN, TW]) for s in range(2)]
        hs = [sb(f"hs{s}", [P, UN, TW]) for s in range(2)]
        x2T = sb("x2T", [P, DC, T])
        tabled = sb("tabled", [P, 1])
        series = sb("series", [P, 2])
        dtr = sb("dtr", [P, T])
        bcs = sb("bcs", [2 * N, T])
        dx = sb("dx", [P, T])
        skip = sb("skip", [P, CH, P])
        st1 = sb("st1", [P, TT, 6])
        mv1 = sb("mv1", [P, TT, 2])
        tiny1 = [sb(f"tiny1{i}", [P, TT]) for i in range(4)]
        st2 = sb("st2", [P, TT, 6])
        mv2 = sb("mv2", [P, TT, 2])
        tiny2 = [sb(f"tiny2{i}", [P, TT]) for i in range(4)]
        lg = sb("lg", [P, TT, E])
        lg2 = sb("lg2", [P, TT, E])
        ranked = [sb(f"ranked{k}", [P, TT, E]) for k in range(2)]
        pw = sb("pw", [P, TT, E])
        le = sb("le", [P, TT, E])
        oh = [sb(f"oh{k}", [P, TT, E]) for k in range(2)]
        sel = sb("sel", [P, TT, E])
        pos = sb("pos", [P, TT, E])
        r1 = sb("r1", [P, TT])
        r2 = sb("r2", [P, TT])
        pk = [sb(f"pk{k}", [P, TT]) for k in range(2)]
        posk = [sb(f"posk{k}", [P, TT]) for k in range(2)]
        idx = [sb(f"idx{k}", [P, TT], I32) for k in range(2)]

        pT = [pb(f"pT{s}", [P, DC, P]) for s in range(TT)]
        pM = [pb(f"pM{s}", [P, 2, T]) for s in range(2)]
        pY = [pb(f"pY{s}", [P, 512]) for s in range(2)]
        pO = pb("pO", [P, D])
        pR = pb("pR", [P, 2, TT + 1, E])

        consts_in = sem("consts_in")
        weights_in = sem("weights_in")
        consts_set = sem("consts_set")
        a_exp = sem("a_exp")
        skip_set = sem("skip_set")
        a_neg = sem("a_neg")
        xf_in = sem("xf_in")
        ln1_step = sem("ln1_step")
        var1 = sem("var1")
        sd1 = sem("sd1")
        xn1 = sem("xn1")
        win_in = [sem(f"win_in{s}") for s in range(2)]
        turned1 = sem("turned1")
        tcopied1 = sem("tcopied1")
        x_mm = sem("x_mm")
        tap3 = sem("tap3")
        conv_step = sem("conv_step")
        xc_ready = sem("xc_ready")
        bc_mm = sem("bc_mm")
        bc_copied = sem("bc_copied")
        bc_stored = sem("bc_stored")
        bc_in = [sem(f"bc_in{i}") for i in range(2 * UPC)]
        dtr_mm = sem("dtr_mm")
        dtr_copied = sem("dtr_copied")
        dt_mm = sem("dt_mm")
        dt_read = sem("dt_read")
        u_ready = sem("u_ready")
        ln_ready = sem("ln_ready")
        sp_step = sem("sp_step")
        delta_ready = sem("delta_ready")
        z_mm = sem("z_mm")
        z_copied = sem("z_copied")
        z_ready = sem("z_ready")
        dx_ready = sem("dx_ready")
        decay = sem("decay")
        inflow = sem("inflow")
        carried = sem("carried")
        scanned = sem("scanned")
        saved = sem("saved")
        weighed = sem("weighed")
        summed = sem("summed")
        gated = sem("gated")
        xb_in = sem("xb_in")
        out_mm = sem("out_mm")
        x1_ready = sem("x1_ready")
        x1_stored = sem("x1_stored")
        back_step = sem("back_step")
        var2 = sem("var2")
        sd2 = sem("sd2")
        xn2 = sem("xn2")
        second_rows = sem("second_rows")
        turned2 = sem("turned2")
        tcopied2 = sem("tcopied2")
        logits_mm = sem("logits_mm")
        exp_in = sem("exp_in")
        exp_out = sem("exp_out")
        sel_ready = sem("sel_ready")
        rank_mm = sem("rank_mm")
        rows_ready = sem("rows_ready")
        scattered = sem("scattered")
        cnt_stored = sem("cnt_stored")
        pool_turn = sem("pool_turn")
        dve_turn = sem("dve_turn")
        sp_turn = sem("sp_turn")

        NCONST, NWEIGHTS = 4, 5
        NSET = 13
        LN1S, BACKS, SPS, LNS = 7, 34, 4, 5
        CONVS = (8 * PAIRS, 12 * PAIRS)

        def conv_base(f, fodd, pair):
            return (CONVS[0] + CONVS[1]) // 2 * (f - fodd) + CONVS[0] * fodd + CONVS[fodd] // PAIRS * pair

        def each_step(eng, emit):
            for s in (-1, 0):
                emit(s, s % 2)
            with eng.Fori(0, (STEPS - 4) // 2) as i:
                emit(2 * i + 1, 1)
                emit(2 * i + 2, 0)
            for s in range(STEPS - 3, STEPS + 1):
                emit(s, s % 2)

        OUT_SLOTS = (2, 4, 5, 6)

        def has(s):
            if not isinstance(s, int):
                return True, True, True, True
            return 0 <= s < STEPS, s + 1 < STEPS, s + 2 < STEPS, s >= 1

        block = ctx.enter_context(nc.Block())

        @block.sync
        def _(sp):
            def hold(sem_, value):
                if not isinstance(value, int) or value > 0:
                    sp.wait_ge(sem_, value)
                    if not isinstance(value, int):
                        sp.sem_inc(sp_turn, 1)

            def tokens(ap, s):
                return ap[bass.ds(s * T, T), :].rearrange("(t p) d -> p t d", p=P)

            def step(s, odd):
                scan, front, ln1, back = has(s)
                f, r = s + 1, s - 1

                def load_win(j):
                    sp.dma_start(win[j % 2][:, :, :], w_in[:, :, j * 4 * P:(j + 1) * 4 * P]).then_inc(win_in[j % 2], 16)

                def load_weights():
                    for dst, src in ((wx, w_x), (wdt, w_dt), (wgate, gate), (wout, w_out)):
                        sp.dma_start(dst[tuple([slice(None)] * len(dst.shape))], src).then_inc(weights_in, 16)
                    sp.wait_ge(consts_set, NSET)
                    sp.dma_start(out[TOKENS:TOKENS + P, :], x2T[:, 0:D // T, :]).then_inc(weights_in, 16)

                if front:
                    hold(z_mm, PAIRS * s + 2)
                    load_win(0)
                if back:
                    hold(x1_stored, 16 * r)
                    hold(xn2, TT * r)
                    sp.dma_start(xb[:, :, :], tokens(x, r)).then_inc(xb_in, 16)
                if front:
                    hold(z_mm, PAIRS * s + 4)
                    load_win(1)
                if isinstance(s, int) and s < 0:
                    load_weights()
                if ln1:
                    hold(turned1, TT * f + TT)
                    sp.dma_start(xf[:, :, :], tokens(x, s + 2)).then_inc(xf_in, 16)
                if front:
                    hold(x_mm, PAIRS * f + 2)
                    load_win(2)
                    hold(x_mm, PAIRS * f + 4)
                    load_win(3)
                if back:
                    hold(x1_ready, TT * r + TT)
                    sp.dma_start(tokens(out, r), xb[:, :, :]).then_inc(x1_stored, 16)
                if front:
                    hold(bc_copied, f + 1)
                    for i in range(2 * UPC):
                        hold(bc_in[i], 16 * f)
                    sp.dma_start(bc_d, bcs[:, :]).then_inc(bc_stored, 16)
                    hold(bc_stored, 16 * f + 16)
                    for g in range(UPC):
                        for i, used in ((2 * g, inflow), (2 * g + 1, weighed)):
                            hold(used, SLOTS * s + SLOTS - UPC + g + 1)
                            lo = (i % 2) * N + g * UN
                            sp.dma_start(bc[:, lo:lo + UN, :],
                                         bc_d[lo:lo + UN, :].rearrange("(a n) t -> a n t", a=1).to_broadcast([P, UN, T]))\
                              .then_inc(bc_in[i], 16)

            sp.dma_start(xf[:, :, :], tokens(x, 0)).then_inc(xf_in, 16)
            for dst, src in ((convw, conv_w), (dtb, dt_bias), (dpar, d_par), (aneg, a_log)):
                sp.dma_start(dst[tuple([slice(None)] * len(dst.shape))], src).then_inc(consts_in, 16)
            each_step(sp, step)
            sp.wait_ge(back_step, BACKS * STEPS)
            sp.dma_start(cnt_d, ebase[0:1, :]).then_inc(cnt_stored, 16)
            sp.wait_ge(cnt_stored, 16)
            sp.wait_ge(x1_stored, 16 * STEPS)
            sp.wait_ge(consts_in, 16 * NCONST)
            sp.wait_ge(weights_in, 16 * NWEIGHTS)

        @block.gpsimd
        def _(pool):
            pool.memset(x2T[:, 0:D // T, :], 0.0).then_inc(consts_set, 1)
            pool.memset(ident[:, :], 0.0).then_inc(consts_set, 1)
            pool.memset(ones[:, :], 1.0).then_inc(consts_set, 1)
            for s in range(2):
                pool.memset(dA[s][:, :, 0:1], 0.0).then_inc(consts_set, 1)
            for i, v in enumerate((LN1P_SHIFT, LN1P_SMALL)):
                pool.memset(series[:, i:i + 1], v).then_inc(consts_set, 1)
            pool.wait_ge(consts_set, 7)
            pool.affine_select(out=ident[:, :], in_=ident[:, :], compare_op=ALU.not_equal, fill=1.0, base=0,
                               pattern=[[-1, P]], channel_multiplier=1).then_inc(consts_set, 1)
            pool.affine_select(out=before[:, :], in_=ones[:, :], compare_op=ALU.is_gt, fill=0.0, base=0,
                               pattern=[[1, P]], channel_multiplier=-1).then_inc(consts_set, 1)
            pool.iota(iota_e[:, :, :], pattern=[[0, TT], [1, E]], base=0, channel_multiplier=0,
                      allow_small_or_imprecise_dtypes=True).then_inc(consts_set, 1)
            pool.iota(iota_e8[:, :, :], pattern=[[0, TT], [1, E]], base=E, channel_multiplier=0,
                      allow_small_or_imprecise_dtypes=True).then_inc(consts_set, 1)
            pool.iota(ebase[:, :], pattern=[[REGION, E]], base=0, channel_multiplier=0,
                      allow_small_or_imprecise_dtypes=True).then_inc(consts_set, 1)
            pool.iota(tok[:, :], pattern=[[P, TT]], base=0, channel_multiplier=1,
                      allow_small_or_imprecise_dtypes=True).then_inc(consts_set, 1)
            with pool.Fori(0, STEPS) as r:
                pool.wait_ge(rows_ready, r + 1)
                pool.sem_inc(pool_turn, 1)
                pool.wait_ge(second_rows, r + 1)
                pool.sem_inc(pool_turn, 1)
                for k in range(2):
                    for t in range(TT):
                        pool.indirect_dma_start(
                            out=rows_d, out_offset=bass.IndirectOffsetOnAxis(ap=idx[k][:, t:t + 1], axis=0),
                            in_=rows[k][:, t, :], in_offset=None).then_inc(scattered, 16)
            pool.wait_ge(scattered, 16 * 2 * TT * STEPS)

        @block.scalar
        def _(act):
            def step(s, odd):
                scan, front, ln1, back = has(s)
                f, r = s + 1, s - 1
                xcf, szs, szf = xc[1 - odd], sz[odd], sz[1 - odd]

                def decays(u):
                    c, g = u // UPC, u % UPC
                    if u == 0:
                        ge(act, delta_ready, 2 * s + 1)
                    if u == 1:
                        ge(act, delta_ready, 2 * s + 2)
                    ge(act, scanned, SLOTS * s + u - 1)
                    for i in range(UN):
                        e = act.activation(dA[u % 2][:, i, 1:TW], delta[:, c, :], ACT.Exp,
                                           scale=aneg[:, c, g * UN + i:g * UN + i + 1])
                    e.then_inc(decay, 1)

                def copy_z(pair, n, szn):
                    ge(act, z_mm, PAIRS * n + pair + 1)
                    act.activation(szn[:, 2 * pair:2 * pair + 2, :], pM[pair % 2][:, :, :], ACT.Copy).then_inc(z_copied, 1)

                def beside(u):
                    if u == 0 and scan:
                        copy_z(PAIRS - 1, s, szs)
                    if u == 1 and scan:
                        ge(act, z_copied, PAIRS * s + PAIRS)
                        act.activation(szs[:, :, :], szs[:, :, :], ACT.Silu).then_inc(z_ready, 1)
                    if u < PAIRS and front:
                        ge(act, gated, CH * r + 2 * u + 2)
                        ge(act, x_mm, PAIRS * f + u + 1)
                        for h in range(2):
                            c = 2 * u + h
                            act.activation(xcf[:, c, :], pM[u % 2][:, h, :], ACT.Copy, scale=convw[:, c, K - 1:K])\
                               .then_inc(tap3, 1)
                    if u == PAIRS + 1 and front:
                        ge(act, conv_step, conv_base(f, 1 - odd, PAIRS))
                        act.activation(xcf[:, :, :], xcf[:, :, :], ACT.Silu).then_inc(xc_ready, 1)
                    if u == 9 and front:
                        ge(act, bc_mm, f + 1)
                        ge(act, bc_stored, 16 * f)
                        act.activation(bcs[:, :], pM[0][0:2 * N, 0, :], ACT.Copy).then_inc(bc_copied, 1)
                    if u == 8 and back:
                        ge(act, var2, r + 1)
                        act.activation(tiny2[1][:, :], tiny2[0][:, :], ACT.Sqrt).then_inc(sd2, 1)
                    if u == 10 and front:
                        ge(act, dtr_mm, f + 1)
                        act.activation(dtr[:, :], pM[1][:, 0, :], ACT.Copy).then_inc(dtr_copied, 1)
                    if u in (11, 12) and front:
                        half = u - 11
                        ge(act, delta_ready, 2 * f)
                        ge(act, dt_mm, 2 * f + half + 1)
                        for q in range(4):
                            c = 4 * half + q
                            ps, col = pM[q // 2][:, q % 2, :], slice(c * T, (c + 1) * T)
                            act.activation(usp[:, col], ps, ACT.Abs, bias=dtb[:, c:c + 1])
                            i = act.activation(vsp[:, col], ps, ACT.Identity, bias=dtb[:, c:c + 1])
                        i.then_inc(dt_read, 1)
                    if u == 10 and back:
                        ge(act, logits_mm, r)
                        for t in range(TT):
                            ge(act, turned2, TT * r + t + 1)
                            act.activation(x2T[:, :, t * P:(t + 1) * P], pT[t][:, :, :], ACT.Copy).then_inc(tcopied2, 1)
                    if u == 12 and front:
                        ge(act, dt_read, 2 * f + 2)
                        act.activation(usp[:, :], usp[:, :], ACT.Exp, scale=-1.0).then_inc(u_ready, 1)
                    if u == 12 and back:
                        ge(act, exp_in, r + 1)
                        act.activation(le[:, :, :], le[:, :, :], ACT.Exp).then_inc(exp_out, 1)
                    if u == 14 and ln1:
                        ge(act, var1, s + 3)
                        act.activation(tiny1[1][:, :], tiny1[0][:, :], ACT.Sqrt).then_inc(sd1, 1)
                    if 13 <= u <= 15 and front:
                        copy_z(u - 13, f, szf)
                    if u == 13 and back:
                        ge(act, xn2, TT * r + TT)
                        ge(act, scattered, 16 * 2 * TT * r)
                        act.activation(rows[1][:, :, 0:D], rows[0][:, :, 0:D], ACT.Copy).then_inc(second_rows, 1)

                if front:
                    ge(act, z_mm, PAIRS * s)
                    for t in range(TT):
                        ge(act, turned1, TT * f + t + 1)
                        act.activation(xnT[1 - odd][:, :, t * P:(t + 1) * P], pT[t][:, :, :], ACT.Copy).then_inc(tcopied1, 1)
                if scan:
                    decays(0)
                for u in range(SLOTS):
                    if scan and u + 1 < SLOTS:
                        decays(u + 1)
                    if u < SLOTS - 1:
                        beside(u)
                if front:
                    dflat = delta[:, :, :].rearrange("p c t -> p (c t)")

                    def series_parts(j):
                        ge(act, scanned, SLOTS * s + SLOTS - 1 + j)
                        part = usp[:, j * CH // 2 * T:(j + 1) * CH // 2 * T].rearrange("p (c t) -> p c t", t=T)
                        act.activation(dA[j][:, 0:CH // 2, 1:TW], part, ACT.Square, bias=series[:, 0:1], scale=LN1P_SLOPE)\
                           .then_inc(ln_ready, 1)
                        act.activation(dA[j][:, CH // 2:CH, 1:TW], part, ACT.Relu, bias=series[:, 1:2], scale=-1.0)\
                           .then_inc(ln_ready, 1)

                    ge(act, u_ready, f + 1)
                    series_parts(0)
                    ge(act, decay, SLOTS * f)
                    ge(act, dx_ready, CH * f)
                    act.activation(dflat, usp[:, :], ACT.Ln, bias=ones[:, 0:1]).then_inc(ln_ready, 1)
                    series_parts(1)
                beside(SLOTS - 1)
                if front:
                    act.activation(tabled[:, :], ones[:, 0:1], ACT.Exp)

            act.wait_ge(var1, 1)
            act.activation(tiny1[1][:, :], tiny1[0][:, :], ACT.Sqrt).then_inc(sd1, 1)
            act.wait_ge(consts_in, 16 * NCONST)
            act.wait_ge(consts_set, NSET)
            act.activation(aneg[:, :, :], aneg[:, :, :], ACT.Exp).then_inc(a_exp, 1)
            for c in range(CH):
                act.activation(skip[:, c, :], ident[:, :], ACT.Copy, scale=dpar[:, c:c + 1]).then_inc(skip_set, 1)
            act.wait_ge(a_neg, 1)
            each_step(act, step)

        @block.tensor
        def _(pe):
            def step(s, odd):
                scan, front, ln1, back = has(s)
                f, r = s + 1, s - 1
                xcf, szr = xc[1 - odd], sz[1 - odd]

                def project(ps, rowsT, wcol, j, h):
                    for d in range(DC):
                        m = pe.matmul(ps[:, h, :], win[j % 2][:, d, wcol:wcol + P], rowsT[:, d, :],
                                      start=d == 0, stop=d == DC - 1)
                    return m

                def z_pair(pair, n, rowsT):
                    if pair >= 2:
                        ge(pe, z_copied, PAIRS * n + pair - 1)
                    else:
                        ge(pe, dt_read, 2 * n + 2)
                    ge(pe, win_in[pair // 2], 16 * (2 * n + 2))
                    for h in range(2):
                        m = project(pM[pair % 2], rowsT, (pair % 2 * 2 + h) * P, 2 + pair // 2, h)
                    m.then_inc(z_mm, 1)

                def beside(u):
                    if u == 0 and front:
                        ge(pe, xn1, TT * f + TT)
                        ge(pe, tcopied2, TT * r)
                        for t in range(TT):
                            for d in range(DC):
                                m = pe.transpose(pT[t][:, d, :], xf[:, t, d * P:(d + 1) * P], ident[:, :])
                            m.then_inc(turned1, 1)
                    if u == 0 and scan:
                        z_pair(PAIRS - 1, s, xnT[odd])
                    if u < PAIRS and front:
                        ge(pe, tcopied1, TT * f + TT)
                        if u < 2:
                            ge(pe, z_copied, PAIRS * s + 3 + u)
                        else:
                            ge(pe, conv_step, conv_base(f, 1 - odd, u - 1))
                        j = u // 2
                        ge(pe, win_in[j], 16 * (2 * f + 1))
                        for h in range(2):
                            m = project(pM[u % 2], xnT[1 - odd], (u % 2 * 2 + h) * P, j, h)
                        m.then_inc(x_mm, 1)
                    if u in OUT_SLOTS and back:
                        t, half = OUT_SLOTS.index(u) // 2, OUT_SLOTS.index(u) % 2
                        ge(pe, gated, CH * s)
                        ge(pe, x1_ready, TT * r + t)
                        for c in range(4 * half, 4 * half + 4):
                            m = pe.matmul(pO[:, :], szr[:, c, t * P:(t + 1) * P], wout[:, c, :],
                                          start=c == 0, stop=c == CH - 1)
                        if half:
                            m.then_inc(out_mm, 1)
                    if u == 9 and isinstance(s, int) and s < 0:
                        pe.wait_ge(weights_in, 16 * NWEIGHTS)
                        pe.wait_ge(skip_set, CH)
                    if u == 9 and front:
                        ge(pe, xc_ready, f + 1)
                        for c in range(CH):
                            m = pe.matmul(pM[0][0:2 * N, 0, :], wx[:, c, R:R + 2 * N], xcf[:, c, :],
                                          start=c == 0, stop=c == CH - 1)
                        m.then_inc(bc_mm, 1)
                    if u == 10 and front:
                        for c in range(CH):
                            m = pe.matmul(pM[1][:, 0, :], wx[:, c, 0:R], xcf[:, c, :], start=c == 0, stop=c == CH - 1)
                        m.then_inc(dtr_mm, 1)
                    if u == 11 and back:
                        ge(pe, tcopied2, TT * r + TT)
                        ge(pe, rows_ready, r)
                        for t in range(TT):
                            for d in range(DC):
                                m = pe.matmul(pR[:, 0, t, :], x2T[:, d, t * P:(t + 1) * P], wgate[:, d, :],
                                              start=d == 0, stop=d == DC - 1)
                        m.then_inc(logits_mm, 1)
                    if u in (11, 12) and front:
                        half = u - 11
                        if half == 0:
                            ge(pe, bc_copied, f + 1)
                            ge(pe, dtr_copied, f + 1)
                        else:
                            ge(pe, dt_read, 2 * f + 1)
                        for q in range(4):
                            c = 4 * half + q
                            m = pe.matmul(pM[q // 2][:, q % 2, :], wdt[:, c * P:(c + 1) * P], dtr[:, :], start=True, stop=True)
                        m.then_inc(dt_mm, 1)
                    if u == 10 and back:
                        ge(pe, tcopied1, TT * (f + 1) if front else TT * STEPS)
                        for t in range(TT):
                            ge(pe, xn2, TT * r + t + 1)
                            for d in range(DC):
                                m = pe.transpose(pT[t][:, d, :], rows[0][:, t, d * P:(d + 1) * P], ident[:, :])
                            m.then_inc(turned2, 1)
                    if 13 <= u <= 15 and front:
                        z_pair(u - 13, f, xnT[1 - odd])
                    if u == 14 and back:
                        ge(pe, sel_ready, r + 1)
                        for t in range(TT + 1):
                            for q in range(min(t + 1, TT)):
                                m = pe.matmul(pR[:, 1, t, :], before[:, :] if q == t else ones[:, :], sel[:, q, :],
                                              start=q == 0, stop=q == min(t, TT - 1))
                        m.then_inc(rank_mm, 1)

                for u in range(SLOTS):
                    beside(u)
                    if scan:
                        c, g = u // UPC, u % UPC
                        if g == 0:
                            ge(pe, gated, CH * s + c - 1)
                            ge(pe, xc_ready, s + 1)
                            pe.matmul(pY[c % 2][:, 0:T], skip[:, c, :], xc[odd][:, c, :], start=True, stop=False)
                        ge(pe, weighed, SLOTS * s + u + 1)
                        for i in range(UN):
                            m = pe.matmul(pY[c % 2][:, 0:T], ident[:, :], hs[u % 2][:, i, 1:TW],
                                          start=False, stop=g == UPC - 1 and i == UN - 1)
                        m.then_inc(summed, 1)

            pe.wait_ge(consts_set, NSET)
            each_step(pe, step)

        @block.vector
        def _(dve):
            class Chain:
                def __init__(self, sem_, base):
                    self.sem, self.base, self.n = sem_, base, 0

                def done(self, ins):
                    self.n += 1
                    ins.then_inc(self.sem, 1)

                def settle(self):
                    ge(dve, self.sem, self.base + self.n)

            def newton(ch, tiny, i):
                ve, sd, rs, nt = tiny
                ch.settle()
                if i == 0:
                    ch.done(dve.reciprocal(rs[:, :], sd[:, :]))
                if i == 1:
                    ch.done(dve.tensor_tensor(nt[:, :], rs[:, :], rs[:, :], ALU.mult))
                if i == 2:
                    ch.done(dve.scalar_tensor_tensor(nt[:, :], nt[:, :], -0.5, ve[:, :], ALU.mult, ALU.mult))
                if i == 3:
                    ch.done(dve.scalar_tensor_tensor(rs[:, :], nt[:, :], 1.5, rs[:, :], ALU.add, ALU.mult))

            def aggregate(ch, st, mv):
                ch.settle()
                dve.sem_inc(dve_turn, 1)
                for t in range(TT):
                    i = dve.bn_aggr(mv[:, t, :], st[:, t, :])
                ch.done(i)

            def normalise(dst, src, mv, tiny, t):
                return dve.tensor_scalar(dst, src, mv[:, t, 0:1], tiny[2][:, t:t + 1], ALU.subtract, ALU.mult)

            ln1_chain = [None]
            LN1_PARTS = 9

            def ln1(n, i):
                if i == 0:
                    ln1_chain[0] = Chain(ln1_step, LN1S * n)
                ch = ln1_chain[0]
                if i < TT:
                    dve.wait_ge(xf_in, 16 * n + 16)
                    ch.done(dve.bn_stats(st1[:, i, :], xf[:, i, :]))
                if i == 2:
                    aggregate(ch, st1, mv1)
                if i == 3:
                    ch.settle()
                    dve.tensor_scalar(tiny1[0][:, :], mv1[:, :, 1], EPS, None, ALU.add).then_inc(var1, 1)
                if i == 4:
                    dve.wait_ge(sd1, n + 1)
                if 4 <= i <= 7:
                    newton(ch, tiny1, i - 4)
                if i == 8:
                    ch.settle()
                    for t in range(TT):
                        normalise(xf[:, t, :], xf[:, t, :], mv1, tiny1, t).then_inc(xn1, 1)
                    assert ch.n == LN1S

            def step(s, odd):
                scan, front, ln1_too, back = has(s)
                f, r, fodd = s + 1, s - 1, 1 - odd
                xcs, xcf = xc[odd], xc[1 - odd]
                conv = None
                bk = Chain(back_step, BACKS * r)

                def feed(c):
                    ge(dve, delta_ready, 2 * s + (1 if c < CH // 2 else 2))
                    ge(dve, inflow, SLOTS * s + UPC * c)
                    dve.tensor_tensor(dx[:, :], delta[:, c, :], xcs[:, c, :], ALU.mult).then_inc(dx_ready, 1)

                def unit(u):
                    c, g = u // UPC, u % UPC
                    k = SLOTS * s + u
                    if u == 0:
                        feed(0)
                        ge(dve, bc_in[0], 16 * s + 16)
                    ge(dve, summed, k - 1)
                    row0 = hs[u % 2][:, :, 0:1]
                    if odd:
                        i = dve.tensor_copy(row0, state[:, c, g * UN:(g + 1) * UN].rearrange("p (n a) -> p n a", a=1))
                    else:
                        i = dve.memset(row0, 0.0)
                    i.then_inc(carried, 1)
                    if c == 0:
                        ge(dve, bc_in[2 * g], 16 * s + 16)
                    ge(dve, dx_ready, CH * s + c + 1)
                    dve.tensor_tensor(hs[u % 2][:, :, 1:TW], dx[:, :].rearrange("p (a t) -> p a t", a=1).to_broadcast([P, UN, T]),
                                      bc[:, g * UN:(g + 1) * UN, :], ALU.mult).then_inc(inflow, 1)
                    beside(u, 0)
                    ge(dve, decay, k + 1)
                    ge(dve, carried, k + 1)
                    ge(dve, inflow, k + 1)
                    flat = hs[u % 2][:, :, :].rearrange("p n t -> p (n t)")
                    dve.tensor_tensor_scan(flat, dA[u % 2][:, :, :].rearrange("p n t -> p (n t)"), flat, 0.0,
                                           ALU.mult, ALU.add).then_inc(scanned, 1)
                    if g == UPC - 1 and c + 1 < CH:
                        feed(c + 1)
                    beside(u, 1)
                    ge(dve, scanned, k + 1)
                    if not odd:
                        dve.tensor_copy(state[:, c, g * UN:(g + 1) * UN].rearrange("p (n a) -> p n a", a=1),
                                        hs[u % 2][:, :, T:TW]).then_inc(saved, 1)
                    beside(u, 2)
                    if not odd:
                        ge(dve, saved, SLOTS // 2 * s + u + 1)
                    if c == 0:
                        ge(dve, bc_in[2 * g + 1], 16 * s + 16)
                    dve.tensor_tensor(hs[u % 2][:, :, 1:TW], hs[u % 2][:, :, 1:TW], bc[:, N + g * UN:N + (g + 1) * UN, :],
                                      ALU.mult).then_inc(weighed, 1)
                    beside(u, 3)

                def finish(n, c, nodd):
                    ge(dve, summed, SLOTS * n + UPC * (c + 1))
                    ge(dve, z_ready, n + 1)
                    dve.tensor_tensor(sz[nodd][:, c, :], pY[c % 2][:, 0:T], sz[nodd][:, c, :], ALU.mult).then_inc(gated, 1)

                def convolve(pair, k, halves):
                    nonlocal conv
                    if k == 0:
                        ge(dve, tap3, CH * f + 2 * pair + 2)
                        conv = Chain(conv_step, conv_base(f, fodd, pair))
                    if halves[0] == 0:
                        conv.settle()
                    sh = K - 1 - k
                    for h in halves:
                        c = 2 * pair + h
                        conv.done(dve.scalar_tensor_tensor(xcf[:, c, sh:T], pM[pair % 2][:, h, 0:T - sh], convw[:, c, k:k + 1],
                                                           xcf[:, c, sh:T], ALU.mult, ALU.add))
                        if fodd:
                            conv.done(dve.scalar_tensor_tensor(xcf[:, c, 0:sh], tail[:, c, K - 1 - sh:K - 1], convw[:, c, k:k + 1],
                                                               xcf[:, c, 0:sh], ALU.mult, ALU.add))
                        elif k == 0:
                            conv.done(dve.tensor_copy(tail[:, c, :], pM[pair % 2][:, h, T - K + 1:T]))

                spread = lambda v: v[:, :].rearrange("p (t a) -> p t a", a=1).to_broadcast([P, TT, E])

                def residual(t):
                    ge(dve, xb_in, 16 * r + 16)
                    ge(dve, out_mm, TT * r + t + 1)
                    dve.tensor_tensor(xb[:, t, :], pO[:, :], xb[:, t, :], ALU.add).then_inc(x1_ready, 1)

                def stats2(t):
                    ge(dve, x1_ready, TT * r + t + 1)
                    bk.done(dve.bn_stats(st2[:, t, :], xb[:, t, :]))

                def route(i):
                    bk.settle()
                    if i == 0:
                        ge(dve, logits_mm, r + 1)
                        bk.done(dve.tensor_copy(lg[:, :, :], pR[:, 0, 0:TT, :]))
                    k, src = (0, lg) if i < 7 else (1, lg2)
                    if i in (1, 7):
                        bk.done(dve.tensor_reduce(r1[:, :], src[:, :, :], AXX, ALU.max))
                    if i == 2:
                        dve.tensor_tensor(le[:, :, :], lg[:, :, :], spread(r1), ALU.subtract).then_inc(exp_in, 1)
                    if i in (2, 8):
                        bk.done(dve.tensor_tensor(oh[k][:, :, :], src[:, :, :], spread(r1), ALU.is_equal))
                    if i in (3, 9):
                        bk.done(dve.scalar_tensor_tensor(oh[k][:, :, :], oh[k][:, :, :], -float(E), iota_e8[:, :, :],
                                                         ALU.mult, ALU.add))
                    if i in (4, 10):
                        bk.done(dve.tensor_reduce(r1[:, :], oh[k][:, :, :], AXX, ALU.min))
                    if i in (5, 11):
                        bk.done(dve.tensor_tensor(oh[k][:, :, :], iota_e[:, :, :], spread(r1), ALU.is_equal))
                    if i == 6:
                        bk.done(dve.scalar_tensor_tensor(lg2[:, :, :], oh[0][:, :, :], -3.0e38, lg[:, :, :],
                                                         ALU.mult, ALU.add))
                    if i == 12:
                        dve.tensor_tensor(sel[:, :, :], oh[0][:, :, :], oh[1][:, :, :], ALU.add).then_inc(sel_ready, 1)

                    if i == 7:
                        ge(dve, exp_out, r + 1)
                        bk.done(dve.tensor_reduce(r2[:, :], le[:, :, :], AXX, ALU.add))
                    if i == 8:
                        bk.done(dve.reciprocal(r2[:, :], r2[:, :]))
                    if i == 9:
                        bk.done(dve.tensor_tensor(le[:, :, :], le[:, :, :], spread(r2), ALU.mult))
                    if i in (10, 12):
                        bk.done(dve.tensor_tensor(pw[:, :, :], le[:, :, :], oh[i // 12][:, :, :], ALU.mult))
                    if i in (11, 13):
                        bk.done(dve.tensor_reduce(pk[i // 13][:, :], pw[:, :, :], AXX, ALU.add))
                    if i == 14:
                        bk.done(dve.tensor_tensor(r2[:, :], pk[0][:, :], pk[1][:, :], ALU.add))
                    if i == 15:
                        bk.done(dve.reciprocal(r2[:, :], r2[:, :]))
                    if i == 16:
                        for k in range(2):
                            dve.tensor_tensor(rows[k][:, :, WCOL], pk[k][:, :], r2[:, :], ALU.mult)
                            dve.tensor_copy(rows[k][:, :, TOKCOL], tok[:, :])

                    if i == 14:
                        ge(dve, rank_mm, r + 1)
                        base = ebase[:, :].rearrange("p (a e) -> p a e", a=1).to_broadcast([P, TT, E])
                        bk.done(dve.tensor_tensor(pos[:, :, :], pR[:, 1, 0:TT, :], base, ALU.add))
                    if i == 15:
                        for k in range(2):
                            bk.done(dve.tensor_tensor(ranked[k][:, :, :], pos[:, :, :], oh[k][:, :, :], ALU.mult))
                        bk.done(dve.tensor_tensor(ebase[:, :], ebase[:, :], pR[:, 1, TT, :], ALU.add))
                    if i == 16:
                        for k in range(2):
                            bk.done(dve.tensor_reduce(posk[k][:, :], ranked[k][:, :, :], AXX, ALU.add))
                    if i == 17:
                        for k in range(2):
                            dve.tensor_copy(idx[k][:, :], posk[k][:, :])
                        dve.tensor_scalar(tok[:, :], tok[:, :], float(T), None, ALU.add).then_inc(rows_ready, 1)
                        assert bk.n == BACKS, bk.n

                def softplus(part):
                    half = lambda v, j: v[:, j * CH // 2 * T:(j + 1) * CH // 2 * T].rearrange("p (c t) -> p c t", t=T)
                    for j in range(2):
                        own = delta[:, j * CH // 2:(j + 1) * CH // 2, :]
                        if part == 0:
                            ge(dve, ln_ready, LNS * f + (3 if j == 0 else LNS))
                            dve.scalar_tensor_tensor(half(usp, j), dA[j][:, 0:CH // 2, 1:TW], LN1P_REST, half(usp, j),
                                                     ALU.add, ALU.mult).then_inc(sp_step, 1)
                        if part == 1:
                            ge(dve, sp_step, SPS * f + 1 + j)
                            dve.sem_inc(dve_turn, 1)
                            dve.copy_predicated(own, dA[j][:, CH // 2:CH, 1:TW].bitcast(I32), half(usp, j)).then_inc(sp_step, 1)
                        if part == 2:
                            ge(dve, sp_step, SPS * f + 3 + j)
                            dve.scalar_tensor_tensor(own, half(vsp, j), 0.0, own, ALU.max, ALU.add).then_inc(delta_ready, 1)

                def beside(u, g):
                    at = (u, g)
                    c = u // UPC
                    if scan and u % UPC == 0 and c >= 1 and g == 3:
                        finish(s, c - 1, odd)
                    if back and at == (0, 3):
                        finish(r, CH - 1, fodd)
                    if 1 <= u <= PAIRS and front:
                        if g == 1:
                            convolve(u - 1, 1, (0,))
                        if g == 2:
                            convolve(u - 1, 1, (1,))
                        if g == 3:
                            convolve(u - 1, 2, (0, 1))
                    if u < PAIRS and front and g == 3:
                        convolve(u, 0, (0, 1))
                    if back:
                        if at == (5, 0):
                            residual(0)
                        if at == (6, 0):
                            stats2(0)
                        if at == (7, 0):
                            residual(1)
                        if at == (7, 1):
                            stats2(1)
                        if at == (7, 3):
                            aggregate(bk, st2, mv2)
                        if at == (8, 0):
                            bk.settle()
                            dve.tensor_scalar(tiny2[0][:, :], mv2[:, :, 1], EPS, None, ALU.add).then_inc(var2, 1)
                        if at == (8, 3):
                            ge(dve, sd2, r + 1)
                            newton(bk, tiny2, 0)
                        if at in ((9, 0), (9, 1), (9, 3)):
                            newton(bk, tiny2, 1 + (0, 1, 3).index(g))
                        if at == (10, 0):
                            bk.settle()
                            ge(dve, scattered, 16 * 2 * TT * r)
                            for t in range(TT):
                                normalise(rows[0][:, t, 0:D], xb[:, t, :], mv2, tiny2, t).then_inc(xn2, 1)
                        if at == (11, 3):
                            route(0)
                        if 12 <= u:
                            route(4 * (u - 12) + g + 1)
                    if ln1_too:
                        if at in ((13, 0), (13, 1), (13, 3), (14, 0)):
                            ln1(s + 2, ((13, 0), (13, 1), (13, 3), (14, 0)).index(at))
                        if u == 15:
                            ln1(s + 2, 4 + g)

                for u in range(SLOTS):
                    if scan:
                        unit(u)
                    else:
                        for g in range(4):
                            beside(u, g)
                if ln1_too:
                    ln1(s + 2, 8)
                if front:
                    softplus(0)
                if back:
                    route(17)
                if front:
                    softplus(1)
                    softplus(2)

            for i in range(LN1_PARTS):
                ln1(0, i)
            dve.wait_ge(a_exp, 1)
            dve.wait_ge(consts_set, NSET)
            dve.tensor_scalar(aneg[:, :, :], aneg[:, :, :], -1.0, None, ALU.mult).then_inc(a_neg, 1)
            dve.wait_ge(consts_in, 16 * NCONST)
            each_step(dve, step)


def experts(nc, w1, w2, w3, out, rows_d, cnt_d):
    with ExitStack() as ctx:
        sb = lambda name, shape, dt=F32: ctx.enter_context(nc.sbuf_tensor(name, shape, dt))
        pb = lambda name, shape: ctx.enter_context(nc.psum_tensor(name, shape, F32))
        sem = lambda name: ctx.enter_context(nc.semaphore(name))

        w1s = sb("w1s", [P, DC, M])
        w3s = sb("w3s", [P, DC, M])
        w2s = sb("w2s", [P, MK, D])
        ident = sb("ident2", [P, P])
        xr = sb("xr", [P, RW])
        xT = sb("xT", [P, DC, P])
        gate = [sb(f"gate{s}", [P, 512]) for s in range(2)]
        hh = sb("hh", [P, M])
        hT = sb("hT", [P, MK, P])
        wrow = sb("wrow", [P, 1])
        trow = sb("trow", [P, 1], I32)
        ow = sb("ow", [P, D])
        pad = sb("pad", [P, RW])
        ptok = sb("ptok", [P, 1])
        ends = sb("ends", [1, E])
        cnt = sb("cnt", [1, E])
        ci = sb("ci", [1, E], I32)
        tiles = sb("tiles", [1, E])
        ebase = sb("ebase2", [1, E])
        tnum = sb("tnum", [1, NT, E])
        over = sb("over", [1, NT, E])
        ex = sb("ex", [1, NT])
        used = sb("used", [1, NT])
        tn = sb("tn", [1, NT])
        first = sb("first", [1, NT])
        one8 = sb("one8", [1, E])
        row_i = sb("row_i", [1, NT], I32)
        ex_i = sb("ex_i", [1, NT], I32)
        load_i = sb("load_i", [1, NT], I32)
        n_i = sb("n_i", [1, 3], I32)
        pad_i = sb("pad_i", [1, E + 1], I32)

        pA = [pb(f"pA{s}", [P, 512]) for s in range(2)]
        pB = [pb(f"pB{s}", [P, 512]) for s in range(2)]
        pH = [pb(f"pH{s}", [P, 4, P]) for s in range(2)]
        pX = pb("pX", [P, DC, P])
        pO = pb("pD", [P, D])

        cnt_in = sem("cnt_in")
        set_up = sem("set_up")
        plan = sem("plan")
        padded = sem("padded")
        x_in = sem("x_in2")
        w13_in = [sem(f"w13_in{q}") for q in range(NQ)]
        w2_in = [sem(f"w2_in{q}") for q in range(NQ)]
        x_turned = sem("x_turned")
        x_copied = sem("x_copied")
        meta = sem("meta")
        up_mm = sem("up_mm")
        silu = sem("silu")
        h_ready = sem("h_ready")
        h_turned = sem("h_turned")
        h_copied = sem("h_copied")
        down_mm = sem("down_mm")
        ow_ready = sem("ow_ready")
        added = sem("added")
        turn = sem("turn2")

        PLAN, PLAN_PAD = 21, 3

        def tiles_filled(eng):
            eng.wait_ge(plan, PLAN)
            return eng.value_load(n_i[0:1, 0:1], min_val=NT_SURE, max_val=NT)

        block = ctx.enter_context(nc.Block())

        @block.gpsimd
        def _(pool):
            pool.memset(ident[:, :], 0.0).then_inc(set_up, 1)
            pool.memset(pad[:, :], 0.0).then_inc(set_up, 1)
            pool.memset(one8[:, :], 1.0).then_inc(set_up, 1)
            pool.wait_ge(set_up, 3)
            pool.affine_select(out=ident[:, :], in_=ident[:, :], compare_op=ALU.not_equal, fill=1.0, base=0,
                               pattern=[[-1, P]], channel_multiplier=1).then_inc(set_up, 1)
            pool.iota(ptok[:, :], pattern=[[0, 1]], base=PADTOK, channel_multiplier=1,
                      allow_small_or_imprecise_dtypes=True).then_inc(set_up, 1)
            pool.iota(tnum[:, :, :], pattern=[[1, NT], [0, E]], base=0, channel_multiplier=0,
                      allow_small_or_imprecise_dtypes=True).then_inc(set_up, 1)
            pool.iota(tn[:, :], pattern=[[1, NT]], base=0, channel_multiplier=0,
                      allow_small_or_imprecise_dtypes=True).then_inc(set_up, 1)
            pool.iota(ebase[:, :], pattern=[[REGION, E]], base=0, channel_multiplier=0,
                      allow_small_or_imprecise_dtypes=True).then_inc(set_up, 1)
            def add_rows(t):
                ge(pool, ow_ready, t + 1)
                ge(pool, added, 16 * t)
                pool.sem_inc(turn, 1)
                pool.indirect_dma_start(out=out, out_offset=bass.IndirectOffsetOnAxis(ap=trow[:, 0:1], axis=0),
                                        in_=ow[:, :], in_offset=None, compute_op=ALU.add).then_inc(added, 16)

            n = tiles_filled(pool)
            add_rows(0)
            with pool.Fori(1, NT_SURE) as t:
                add_rows(t)
            with pool.Fori(NT_SURE, NT) as t:
                with pool.If(t < n):
                    add_rows(t)
            pool.wait_ge(added, n * 16)

        @block.sync
        def _(sp):
            sp.dma_start(cnt[:, :], cnt_d).then_inc(cnt_in, 16)

            def load_rows(t):
                r = sp.value_load(row_i[0:1, bass.ds(t, 1)], min_val=0, max_val=DUMMY)
                sp.dma_start(xr[:, :], rows_d[bass.ds(r, P), :]).then_inc(x_in, 16)

            def load_up(q, e, c=None):
                lo, n = WCH[q]
                for ws, w in ((w1s, w1), (w3s, w3)):
                    src = w[bass.ds(e * D, D), lo:lo + n].rearrange("(c p) m -> p c m", p=P)
                    if c is None:
                        sp.dma_start(ws[:, :, lo:lo + n], src).then_inc(w13_in[q], 16)
                    else:
                        sp.dma_start(ws[:, :, lo:lo + n], src, cond=c, bounds_check="skip_entire_dma")\
                          .then_inc(w13_in[q], 16)

            def load_down(q, e, c=None):
                lo, n = WCH[q][0] // P, WCH[q][1] // P
                src = w2[bass.ds(e * M + lo * P, n * P), :].rearrange("(k p) d -> p k d", p=P)
                if c is None:
                    sp.dma_start(w2s[:, lo:lo + n, :], src).then_inc(w2_in[q], 16)
                else:
                    sp.dma_start(w2s[:, lo:lo + n, :], src, cond=c, bounds_check="skip_entire_dma")\
                      .then_inc(w2_in[q], 16)

            n = tiles_filled(sp)
            e0 = sp.value_load(ex_i[0:1, 0:1], min_val=0, max_val=E - 1)
            load_up(0, e0)
            sp.wait_ge(padded, 16 * (E + 1))
            load_rows(0)
            for q in range(1, NQ):
                load_up(q, e0)
            for q in range(NQ):
                load_down(q, e0)
            def load_next(t):
                sp.wait_ge(x_turned, t + 1)
                sp.wait_ge(meta, t + 1)
                load_rows(t + 1)
                e1 = sp.value_load(ex_i[0:1, bass.ds(t + 1, 1)], min_val=0, max_val=E - 1)
                new = sp.value_load(load_i[0:1, bass.ds(t + 1, 1)], min_val=0, max_val=1)
                for q in range(NQ):
                    sp.wait_ge(up_mm, NQ * t + q + 1)
                    load_up(q, e1, new > 0)
                for q in range(NQ):
                    sp.wait_ge(down_mm, NQ * t + q + 1)
                    load_down(q, e1, new > 0)

            with sp.Fori(0, NT_SURE) as t:
                load_next(t)
            with sp.Fori(NT_SURE, NT - 1) as t:
                with sp.If(t < n):
                    load_next(t)
            down_loads = sp.value_load(n_i[0:1, 1:2], min_val=16 * NT_SURE, max_val=16 * NT)
            up_loads = sp.value_load(n_i[0:1, 2:3], min_val=32 * NT_SURE, max_val=32 * NT)
            for q in range(NQ):
                for sem_, value in ((w13_in[q], up_loads), (w2_in[q], down_loads)):
                    sp.wait_ge(sem_, value)
                    sp.sem_inc(turn, 1)

        @block.scalar
        def _(act):
            def tile(t, last):
                def silu_q(q):
                    n = WCH[q][1]
                    act.wait_ge(up_mm, NQ * t + q + 1)
                    ge(act, h_ready, NQ * t + max(q - 1, 0))
                    act.activation(gate[q % 2][:, 0:n], pA[q % 2][:, 0:n], ACT.Silu).then_inc(silu, 1)

                def copy_q(q):
                    lo, n = WCH[q][0] // P, WCH[q][1] // P
                    act.wait_ge(h_turned, NQ * t + q + 1)
                    act.activation(hT[:, lo:lo + n, :], pH[q % 2][:, 0:n, :], ACT.Copy).then_inc(h_copied, 1)

                silu_q(0)
                for q in range(1, NQ):
                    silu_q(q)
                    copy_q(q - 1)
                if not last:
                    act.wait_ge(x_turned, t + 2)
                    act.activation(xT[:, :, :], pX[:, :, :], ACT.Copy).then_inc(x_copied, 1)
                copy_q(NQ - 1)

            act.wait_ge(plan, PLAN_PAD)
            with act.Fori(0, E + 1) as e:
                r = act.value_load(pad_i[0:1, bass.ds(e, 1)], min_val=0, max_val=DUMMY)
                act.dma_start(rows_d[bass.ds(r, P), :], pad[:, :]).then_inc(padded, 16)
            act.wait_ge(x_turned, 1)
            act.activation(xT[:, :, :], pX[:, :, :], ACT.Copy).then_inc(x_copied, 1)
            n = tiles_filled(act)
            tile(0, False)
            with act.Fori(1, NT_SURE) as t:
                tile(t, False)
            with act.Fori(NT_SURE, NT - 1) as t:
                with act.If(t < n):
                    tile(t, False)
            with act.If(n > NT - 1):
                tile(NT - 1, True)

        @block.tensor
        def _(pe):
            def turn_rows(t):
                pe.wait_ge(x_in, 16 * t + 16)
                for d in range(DC):
                    m = pe.transpose(pX[:, d, :], xr[:, d * P:(d + 1) * P], ident[:, :])
                m.then_inc(x_turned, 1)

            def tile(t, last):
                def up(q):
                    lo, n = WCH[q]
                    pe.wait_ge(w13_in[q], 32 * t + 32)
                    ge(pe, h_ready, NQ * t + max(q - 1, 0))
                    for ps, ws in ((pA, w1s), (pB, w3s)):
                        for d in range(DC):
                            m = pe.matmul(ps[q % 2][:, 0:n], xT[:, d, :], ws[:, d, lo:lo + n],
                                          start=d == 0, stop=d == DC - 1)
                    m.then_inc(up_mm, 1)

                def turn_h(q):
                    pe.wait_ge(h_ready, NQ * t + q + 1)
                    ge(pe, h_copied, NQ * t + max(q - 1, 0))
                    lo, n = WCH[q][0] // P, WCH[q][1] // P
                    for k in range(n):
                        m = pe.transpose(pH[q % 2][:, k, :], hh[:, (lo + k) * P:(lo + k + 1) * P], ident[:, :])
                    m.then_inc(h_turned, 1)

                def down(q):
                    lo, n = WCH[q][0] // P, WCH[q][1] // P
                    pe.wait_ge(h_copied, NQ * t + q + 1)
                    pe.wait_ge(w2_in[q], 16 * t + 16)
                    for k in range(lo, lo + n):
                        m = pe.matmul(pO[:, :], hT[:, k, :], w2s[:, k, :], start=k == 0, stop=k == MK - 1)
                    m.then_inc(down_mm, 1)

                pe.wait_ge(x_copied, t + 1)
                up(0)
                for q in range(1, NQ):
                    up(q)
                    turn_h(q - 1)
                if not last:
                    turn_rows(t + 1)
                ge(pe, ow_ready, t)
                for q in range(NQ - 1):
                    down(q)
                turn_h(NQ - 1)
                down(NQ - 1)

            pe.wait_ge(set_up, 8)
            turn_rows(0)
            n = tiles_filled(pe)
            tile(0, False)
            with pe.Fori(1, NT_SURE) as t:
                tile(t, False)
            with pe.Fori(NT_SURE, NT - 1) as t:
                with pe.If(t < n):
                    tile(t, False)
            with pe.If(n > NT - 1):
                tile(NT - 1, True)

        @block.vector
        def _(dve):
            count = [0]

            def link(ins):
                count[0] += 1
                ins.then_inc(plan, 1)
                dve.wait_ge(plan, count[0])

            dve.wait_ge(set_up, 8)
            dve.wait_ge(cnt_in, 16)
            link(dve.tensor_copy(pad[:, TOKCOL:TOKCOL + 1], ptok[:, :]))
            link(dve.tensor_copy(pad_i[:, 0:E], cnt[:, :]))
            link(dve.memset(pad_i[:, E:E + 1], DUMMY))
            link(dve.tensor_tensor(ends[:, :], cnt[:, :], ebase[:, :], ALU.subtract))
            link(dve.tensor_scalar(ci[:, :], ends[:, :], float(P - 1), None, ALU.add))
            link(dve.tensor_scalar(ci[:, :], ci[:, :], P.bit_length() - 1, None, ALU.logical_shift_right))
            link(dve.tensor_copy(tiles[:, :], ci[:, :]))
            link(dve.tensor_tensor_scan(ends[:, :], one8[:, :], tiles[:, :], 0.0, ALU.mult, ALU.add))
            link(dve.tensor_copy(n_i[:, 0:1], ends[:, E - 1:E]))
            link(dve.tensor_scalar(first[:, 0:1], ends[:, E - 1:E], 1.0, float(NT), ALU.add, ALU.min))
            dve.tensor_scalar(n_i[:, 1:2], first[:, 0:1], 16.0, None, ALU.mult)
            link(dve.tensor_scalar(n_i[:, 2:3], first[:, 0:1], 32.0, None, ALU.mult))
            wide = lambda v: v[:, :].rearrange("p (a e) -> p a e", a=1).to_broadcast([1, NT, E])
            link(dve.tensor_tensor(over[:, :, :], tnum[:, :, :], wide(ends), ALU.is_ge))
            link(dve.tensor_reduce(ex[:, :], over[:, :, :], AXX, ALU.add))
            link(dve.tensor_tensor(over[:, :, :], over[:, :, :], wide(tiles), ALU.mult))
            link(dve.tensor_reduce(used[:, :], over[:, :, :], AXX, ALU.add))
            link(dve.tensor_tensor(used[:, :], tn[:, :], used[:, :], ALU.subtract))
            link(dve.tensor_scalar(used[:, :], used[:, :], float(P), None, ALU.mult))
            link(dve.scalar_tensor_tensor(used[:, :], ex[:, :], float(REGION), used[:, :], ALU.mult, ALU.add))
            dve.tensor_scalar(row_i[:, :], used[:, :], float(DUMMY), None, ALU.min)
            link(dve.tensor_scalar(ex[:, :], ex[:, :], float(E - 1), None, ALU.min))
            dve.tensor_copy(ex_i[:, :], ex[:, :])
            dve.tensor_tensor(first[:, 1:NT], ex[:, 1:NT], ex[:, 0:NT - 1], ALU.not_equal)
            link(dve.memset(first[:, 0:1], 1.0))
            link(dve.tensor_copy(load_i[:, :], first[:, :]))
            assert count[0] == PLAN, count[0]

            def tile(t):
                dve.wait_ge(x_in, 16 * t + 16)
                ge(dve, added, 16 * t)
                dve.tensor_copy(trow[:, :], xr[:, TOKCOL:TOKCOL + 1])
                dve.tensor_copy(wrow[:, :], xr[:, WCOL:WCOL + 1]).then_inc(meta, 1)
                for q in range(NQ):
                    lo, n = WCH[q]
                    dve.wait_ge(silu, NQ * t + q + 1)
                    dve.tensor_tensor(hh[:, lo:lo + n], gate[q % 2][:, 0:n], pB[q % 2][:, 0:n], ALU.mult)\
                       .then_inc(h_ready, 1)
                dve.wait_ge(down_mm, NQ * t + NQ)
                dve.wait_ge(meta, t + 1)
                dve.tensor_scalar(ow[:, :], pO[:, :], wrow[:, 0:1], None, ALU.mult).then_inc(ow_ready, 1)

            n = tiles_filled(dve)
            tile(0)
            with dve.Fori(1, NT_SURE) as t:
                tile(t)
            with dve.Fori(NT_SURE, NT) as t:
                with dve.If(t < n):
                    tile(t)


def build(nc, x, w_in, conv_w, w_x, w_dt, dt_bias, a_log, d_par, w_out, gate, w1, w2, w3, out):
    rows_d = nc.dram_tensor("rows_d", (DUMMY + P, RW), F32, kind="Internal").ap()
    bc_d = nc.dram_tensor("bc_d", (2 * N, T), F32, kind="Internal").ap()
    cnt_d = nc.dram_tensor("cnt_d", (1, E), F32, kind="Internal").ap()
    mixer(nc, x, w_in, conv_w, w_x, w_dt, dt_bias, a_log, d_par, w_out, gate, out, rows_d, bc_d, cnt_d)
    experts(nc, w1, w2, w3, out, rows_d, cnt_d)


def kernel(**inputs):
    import concourse.bacc as bacc
    from concourse.bass_utils import run_bass_kernel_spmd

    def chunks(a):
        return a.reshape(-1, P, *a.shape[1:]).swapaxes(0, 1)

    g = {k.removeprefix("L0_attn_").removeprefix("L0_ffn_"): np.asarray(v) for k, v in inputs.items()}
    arrays = {
        "x": g["hidden_states"].reshape(TOKENS, D),
        "w_in": chunks(g["in_proj_w"].T),
        "conv_w": chunks(g["conv1d_w"]),
        "w_x": chunks(g["x_proj_w"].T),
        "w_dt": g["dt_proj_w"].T,
        "dt_bias": chunks(g["dt_proj_bias"]),
        "a_log": chunks(g["A_log"]),
        "d_par": chunks(g["D_param"]),
        "w_out": chunks(g["out_proj_w"].T),
        "gate": chunks(g["gate_w"]),
        "w1": g["w1"].reshape(E * D, M),
        "w2": g["w2"].reshape(E * M, D),
        "w3": g["w3"].reshape(E * D, M),
    }
    nc = bacc.Bacc("TRN2", target_bir_lowering=False, num_devices=1)
    feeds, args = {}, []
    for name, a in arrays.items():
        a = np.ascontiguousarray(a)
        feeds[f"in_{name}"] = a
        args.append(nc.dram_tensor(f"in_{name}", a.shape, mybir.dt.from_np(a.dtype), kind="ExternalInput").ap())
    out = nc.dram_tensor("out_0", (TOKENS + P, D), F32, kind="ExternalOutput").ap()
    build(nc, *args, out)
    r = run_bass_kernel_spmd(nc, [feeds], core_ids=[0])
    return r.results[0]["out_0"][:TOKENS].reshape(B, L, D)
```
